# Optimizing a Trainium2 kernel written in Bass

```python
import numpy as np
import jax
import jax.numpy as jnp

def _softmax(x, axis=-1):
    return jax.nn.softmax(x, axis=axis)

def _gelu(x):
    return jax.nn.gelu(x, approximate=True)

def _silu(x):
    return jax.nn.silu(x)

def _sigmoid(x):
    return jax.nn.sigmoid(x)

def _layernorm(x, axis=-1, eps=1e-05):
    m = jnp.mean(x, axis=axis, keepdims=True)
    v = jnp.var(x, axis=axis, keepdims=True)
    return (x - m) / jnp.sqrt(v + eps)

def _scatter_add(tgt, idx, src, axis=0):
    return tgt.at[idx].add(src)

def _segment_sum(src, seg, n):
    return jax.ops.segment_sum(src, seg, n)
kernel_name = 'mk_xattn_ffn_d1_seqx_r2_bac3b0'

def setup_inputs(seed: int=0):
    np.random.seed(seed)
    _w = jnp.asarray

    def _rec_inputs():
        import jax
        import jax.numpy as jnp
        _rk = jax.random.key(seed)
        x = -0.0002928 + 1 * jax.random.normal(jax.random.fold_in(_rk, 1), (8, 512, 512), jnp.float32)
        _lenS = 512 - jax.random.randint(jax.random.fold_in(_rk, 7), (8,), 0, max(1, 512 // 4) + 1, jnp.int32)
        _lenS2 = 512 - jax.random.randint(jax.random.fold_in(_rk, 8), (8,), 0, max(1, 512 // 4) + 1, jnp.int32)
        _ctx_1024P = jax.random.normal(jax.random.fold_in(_rk, 11), (8, 16, 512), jnp.float32)
        _ctx_1024c = jax.random.dirichlet(jax.random.fold_in(_rk, 511), 0.3 * jnp.ones((16,), jnp.float32), (8, 512))
        _ctx_1024t = jnp.einsum('bsk,bkd->bsd', _ctx_1024c, _ctx_1024P)
        _ctx_1024t = _ctx_1024t * jax.lax.rsqrt(jnp.mean(jnp.square(_ctx_1024t)) + 1e-12) * 0.953939
        ctx_1024 = -1.39393e-06 + 0.999914 * (_ctx_1024t + 0.3 * jax.random.normal(jax.random.fold_in(_rk, 611), (8, 512, 512), jnp.float32))
        return (x, ctx_1024)
    x, ctx_1024 = _rec_inputs()

    def _L0_xattn_setup():
        import jax, jax.numpy as jnp
        import numpy as np
        B, T, N_EMBD, N_HEAD = (2, 1024, 512, 16)
        HEAD = N_EMBD // N_HEAD
        WINDOW = 64
        key = jax.random.key(seed)
        kq, kk, kv, kw = jax.random.split(key, 4)
        q = jax.random.normal(kq, (B, T, N_EMBD), dtype=jnp.float32)
        k = jax.random.normal(kk, (B, T, N_EMBD), dtype=jnp.float32)
        v = jax.random.normal(kv, (B, T, N_EMBD), dtype=jnp.float32)
        W_proj = jax.random.normal(kw, (N_EMBD, N_EMBD), dtype=jnp.float32) * (1.0 / np.sqrt(N_EMBD))
        b_proj = jnp.zeros((N_EMBD,), dtype=jnp.float32)
        return {'q': q, 'k': k, 'v': v, 'W_proj': W_proj, 'b_proj': b_proj}
    _L0_xattn_all = _L0_xattn_setup()
    _L0_xattn_in = {k: v for k, v in _L0_xattn_all.items() if k in ('W_proj', 'b_proj')}
    del _L0_xattn_all

    def _L0_ffn_setup():
        import jax, jax.numpy as jnp
        import numpy as np
        from jax import lax
        T, B, I, M, O = (128, 64, 512, 512, 512)

        def _xavier(key, shape):
            fan_out, fan_in = shape
            limit = float(np.sqrt(6.0 / (fan_in + fan_out)))
            return jax.random.uniform(key, shape, jnp.float32, -limit, limit)
        key = jax.random.key(seed)
        ks = jax.random.split(key, 9)
        x = jax.random.normal(ks[0], (T, B, I), jnp.float32)
        return {'x': x, 'wf': _xavier(ks[1], (M, I)), 'uf': _xavier(ks[2], (M, M)), 'bf': jnp.zeros((M,), jnp.float32), 'wi': _xavier(ks[3], (M, I)), 'ui': _xavier(ks[4], (M, M)), 'bi': jnp.zeros((M,), jnp.float32), 'wc': _xavier(ks[5], (M, I)), 'uc': _xavier(ks[6], (M, M)), 'bc': jnp.zeros((M,), jnp.float32), 'wo': _xavier(ks[7], (O, I)), 'uo': _xavier(ks[8], (O, M)), 'bo': jnp.zeros((O,), jnp.float32), 'in_c': jnp.zeros((M,), jnp.float32)}
    _L0_ffn_all = _L0_ffn_setup()
    _L0_ffn_in = {k: v for k, v in _L0_ffn_all.items() if k in ('wf', 'uf', 'bf', 'wi', 'ui', 'bi', 'wc', 'uc', 'bc', 'wo', 'uo', 'bo', 'in_c')}
    del _L0_ffn_all
    return {'x': x, 'ctx_1024': ctx_1024, 'L0_xattn_W_proj': _L0_xattn_in['W_proj'], 'L0_xattn_b_proj': _L0_xattn_in['b_proj'], 'L0_ffn_wf': _L0_ffn_in['wf'], 'L0_ffn_uf': _L0_ffn_in['uf'], 'L0_ffn_bf': _L0_ffn_in['bf'], 'L0_ffn_wi': _L0_ffn_in['wi'], 'L0_ffn_ui': _L0_ffn_in['ui'], 'L0_ffn_bi': _L0_ffn_in['bi'], 'L0_ffn_wc': _L0_ffn_in['wc'], 'L0_ffn_uc': _L0_ffn_in['uc'], 'L0_ffn_bc': _L0_ffn_in['bc'], 'L0_ffn_wo': _L0_ffn_in['wo'], 'L0_ffn_uo': _L0_ffn_in['uo'], 'L0_ffn_bo': _L0_ffn_in['bo'], 'L0_ffn_in_c': _L0_ffn_in['in_c']}

def reference(x, ctx_1024, L0_xattn_W_proj, L0_xattn_b_proj, L0_ffn_wf, L0_ffn_uf, L0_ffn_bf, L0_ffn_wi, L0_ffn_ui, L0_ffn_bi, L0_ffn_wc, L0_ffn_uc, L0_ffn_bc, L0_ffn_wo, L0_ffn_uo, L0_ffn_bo, L0_ffn_in_c):
    import jax
    import jax.numpy as jnp

    def _L0_xattn_ref(q, k, v, W_proj, b_proj):
        import jax, jax.numpy as jnp
        import numpy as np
        B, T, N_EMBD, N_HEAD = (2, 1024, 512, 16)
        HEAD = N_EMBD // N_HEAD
        WINDOW = 64
        Bsz, Tlen, _ = q.shape
        qh = q.reshape(Bsz, Tlen, N_HEAD, HEAD).transpose(0, 2, 1, 3)
        kh = k.reshape(Bsz, Tlen, N_HEAD, HEAD).transpose(0, 2, 1, 3)
        vh = v.reshape(Bsz, Tlen, N_HEAD, HEAD).transpose(0, 2, 1, 3)
        scale = 1.0 / np.sqrt(HEAD)
        scores = jnp.einsum('bhqd,bhkd->bhqk', qh, kh) * scale
        idx = jnp.arange(Tlen)
        dist = jnp.abs(idx[None, :] - idx[:, None])
        scores = jnp.where(dist[None, None] > WINDOW, -jnp.inf, scores)
        attn = jax.nn.softmax(scores, axis=-1)
        y = jnp.einsum('bhqk,bhkd->bhqd', attn, vh)
        y = y.transpose(0, 2, 1, 3).reshape(Bsz, Tlen, N_EMBD)
        return y @ W_proj.T + b_proj

    def _L0_ffn_ref(x, wf, uf, bf, wi, ui, bi, wc, uc, bc, wo, uo, bo, in_c):
        import jax, jax.numpy as jnp
        import numpy as np
        from jax import lax
        T, B, I, M, O = (128, 64, 512, 512, 512)

        def _xavier(key, shape):
            fan_out, fan_in = shape
            limit = float(np.sqrt(6.0 / (fan_in + fan_out)))
            return jax.random.uniform(key, shape, jnp.float32, -limit, limit)
        batch = x.shape[1]
        c0 = jnp.broadcast_to(in_c, (batch, in_c.shape[0]))

        def step(c, xt):
            ft = jax.nn.sigmoid(xt @ wf.T + c @ uf.T + bf)
            it = jax.nn.sigmoid(xt @ wi.T + c @ ui.T + bi)
            gt = jnp.tanh(xt @ wc.T + c @ uc.T + bc)
            c = ft * c + it * gt
            return (c, None)
        c_final, _ = lax.scan(step, c0, x)
        h = jnp.tanh(jnp.einsum('tbi,oi->tbo', x, wo) + c_final @ uo.T + bo)
        return h
    x = x + _L0_xattn_ref(_layernorm(x, axis=-1), ctx_1024, ctx_1024, L0_xattn_W_proj, L0_xattn_b_proj)
    x = x + _L0_ffn_ref(_layernorm(x, axis=-1), L0_ffn_wf, L0_ffn_uf, L0_ffn_bf, L0_ffn_wi, L0_ffn_ui, L0_ffn_bi, L0_ffn_wc, L0_ffn_uc, L0_ffn_bc, L0_ffn_wo, L0_ffn_uo, L0_ffn_bo, L0_ffn_in_c)
    return x

_drawn_inputs = setup_inputs


def setup_inputs(seed=0):
    import zlib

    import numpy as np

    out = dict(_drawn_inputs(seed))
    spreads = {'L0_xattn_b_proj': (0.0, 0.1),
     'L0_ffn_bf': (0.0, 0.8),
     'L0_ffn_bi': (0.0, 0.783),
     'L0_ffn_bc': (0.0, 0.1),
     'L0_ffn_bo': (0.0, 0.1),
     'L0_ffn_in_c': (0.0, 0.8)}
    factors = {}
    for name, (base, spread) in spreads.items():
        noise = np.random.default_rng([zlib.crc32(name.encode()), seed]).standard_normal(out[name].shape)
        drawn = base * np.exp(spread * noise) if base else spread * noise
        out[name] = jnp.asarray(drawn.astype(out[name].dtype))
    for name, factor in factors.items():
        out[name] = (out[name] * factor).astype(out[name].dtype)
    return out
```

```python
from contextlib import ExitStack

import concourse.bass as bass
from concourse import mybir

F32 = mybir.dt.float32
F32R = mybir.dt.float32r
ALU = mybir.AluOpType
ACT = mybir.ActivationFunctionType
AX = mybir.AxisListType

P = 128
HEAD = 32
HPG = P // HEAD
WINDOW = 64
KEYS = P + 2 * WINDOW
EPS = 1e-5
NEG = -3.0e38
DMA = 16


def bass_xattn_ffn(nc, x, ctx_rows, ctx_t, w_proj, b_proj, w_gates, u_gates, biases, w_out, u_out,
                   b_out, in_c, out, x1_dram):
    B, T, D = x.shape
    TT = T // P
    G = D // P
    SCALE = float(HEAD) ** -0.5
    NG = 3
    UNITS = NG * G
    SLOTS = G * TT
    NSTACK = DMA * HPG * HPG
    KEY0 = [min(max(P * t - WINDOW, 0), T - KEYS) for t in range(TT)]
    VTILES = [[k // P + c if k % P == 0 else TT + k // P + c for c in range(2)] for k in KEY0]
    NV = 2 * TT - 1
    MASK0 = [WINDOW + KEY0[t] - (P * t - WINDOW) for t in range(TT)]
    MASKW = KEYS + 2 * WINDOW

    QUARTERS = UNITS * G
    HEADQ, SLOTQ = (4, 6, 2), 2
    steps = []
    q = 0

    def cells(n):
        nonlocal q
        for _ in range(n):
            if q < QUARTERS:
                steps.append(("cell", q))
                q += 1

    cells(HEADQ[0])
    steps.append(("norm1", 0))
    cells(HEADQ[1])
    steps.append(("prep", 0))
    cells(HEADQ[2])
    for s in range(SLOTS + 1):
        if s > 0:
            steps.append(("turn", s - 1))
        if s < SLOTS:
            steps.append(("score", s))
            if s % TT == 1 and s // TT + 1 < G:
                steps.append(("prep", s // TT + 1))
        else:
            steps.append(("weights", 0))
        cells(SLOTQ // 2)
        if s > 0:
            steps.append(("value", s - 1))
            if (s - 1) % TT == TT - 1:
                steps.append(("norm", (s - 1) // TT))
        cells(SLOTQ // 2)
    cells(QUARTERS - q)
    steps.append(("state", 0))
    for t in range(TT):
        steps.append(("proj", t))
        if t > 0:
            steps.append(("turn2", t - 1))
    steps.append(("turn2", TT - 1))
    attn_kinds = ("norm1", "prep", "turn", "score", "value", "norm", "weights", "proj", "turn2")
    cell_kinds = ("cell", "state")

    chunks = [(g, u, k) for g in range(NG) for u in range(2) for k in range(G)]
    NCH = len(chunks)
    WPS = NCH // (SLOTS - TT)

    with ExitStack() as ctx:
        def sb(name, shape, dt):
            return ctx.enter_context(nc.sbuf_tensor(name, shape, dt))

        def pb(name):
            return ctx.enter_context(nc.psum_tensor(name, [P, 512], F32))

        def sem(name):
            return ctx.enter_context(nc.semaphore(name))

        gate_w = sb("gate_w", [P, NG, 2, 2, G, D], F32R)
        key_stack = sb("key_stack", [P, 2, HPG, T], F32R)
        query_stack = sb("query_stack", [P, HPG, T], F32R)
        x2t_hi = sb("x2t_hi", [P, G, T], F32R)
        x2t_lo = sb("x2t_lo", [P, G, T], F32R)
        xa = sb("xa", [P, G, T], F32)
        state = sb("state", [P, G, T], F32)
        state_hi = sb("state_hi", [P, G, T], F32R)
        state_lo = sb("state_lo", [P, G, T], F32R)
        values = sb("values", [P, 2, NV, P], F32)
        probs = sb("probs", [P, 2, HPG, KEYS], F32)
        probs_t = sb("probs_t", [P, 2 * HPG, P], F32)
        mask = sb("mask", [P, MASKW], F32)
        gate = sb("gate", [P, 2, T], F32)
        stage_hi = sb("stage_hi", [P, T], F32R)
        stage_lo = sb("stage_lo", [P, T], F32)
        xr = sb("xr", [P, 2, D], F32)
        x2 = sb("x2", [P, D], F32)
        recip_sb = x2
        ident = sb("ident", [P, P], F32)
        rowsum = sb("rowsum", [P, TT, HPG], F32)
        recip = sb("recip", [P, TT, P], F32)
        negmax = sb("negmax", [P, 2, HPG], F32)
        rowmax = sb("rowmax", [P, 2, HPG], F32)
        bias = sb("bias", [P, NG, G], F32)
        c0 = sb("c0", [P, G], F32)
        half = sb("half", [P, TT], F32)
        st1 = sb("st1", [P, TT, 6], F32)
        mv1 = sb("mv1", [P, TT, 2], F32)
        ve1 = sb("ve1", [P, TT], F32)
        rs1 = sb("rs1", [P, TT], F32)
        st2 = sb("st2", [P, 6], F32)
        mv2 = sb("mv2", [P, 2], F32)
        ve2 = sb("ve2", [P, 1], F32)
        rs2 = sb("rs2", [P, 1], F32)
        bp_row = sb("bp_row", [P, D], F32)

        ps_s = [pb("ps_s0"), pb("ps_s1")]
        ps_t = [pb("ps_t0"), pb("ps_t1")]
        ps_v = pb("ps_v")
        ps_x = pb("ps_x")
        ps_d = [pb("ps_d0"), pb("ps_d1")]
        ps_proj = ps_s + ps_t

        x_in = sem("x_in"); k_in = sem("k_in"); v_in = [sem("v_in0"), sem("v_in1")]
        k_stacked = sem("k_stacked"); q_stacked = [sem("q_stacked0"), sem("q_stacked1")]
        xr_in = [sem("xr_in0"), sem("xr_in1")]; x1_out = [sem("x1_out0"), sem("x1_out1")]
        w_in = [sem(f"w_in{i}") for i in range(G)]
        const_in = sem("const_in"); proj_in = sem("proj_in"); bp_in = sem("bp_in")
        consts = sem("consts"); rstd1 = sem("rstd1"); rstd2 = sem("rstd2"); xr_ready = sem("xr_ready")
        stat1 = sem("stat1"); aggr1 = sem("aggr1"); var1 = sem("var1"); ln1 = sem("ln1")
        k_lo = sem("k_lo"); q_lo = sem("q_lo"); masked = sem("masked"); nmax = sem("nmax")
        turned_b = sem("turned_b"); inv = sem("inv"); attn_t = sem("attn_t")
        x1_done = sem("x1_done"); stat2 = sem("stat2"); aggr2 = sem("aggr2"); var2 = sem("var2")
        x2_done = sem("x2_done"); x2_lo = sem("x2_lo"); w_lo = sem("w_lo")
        in_gate = sem("in_gate"); kept = sem("kept"); cell = sem("cell"); c_lo = sem("c_lo")
        bias_half = sem("bias_half"); c_init = sem("c_init")
        k_hi = sem("k_hi"); q_hi = sem("q_hi"); expd = sem("expd"); turned_a = sem("turned_a")
        recip_out = sem("recip_out"); x2_hi = sem("x2_hi"); w_hi = sem("w_hi")
        gated = sem("gated"); c_hi = sem("c_hi")
        q_turned = sem("q_turned"); scored = sem("scored"); turned = sem("turned")
        valued = sem("valued"); spread = sem("spread"); projected = sem("projected")
        x2_turned = sem("x2_turned"); gate_sum = sem("gate_sum")
        passed = sem("passed")
        e = {n: sem("e_" + n) for n in (
            "raw_in", "hi", "lo", "base_mm", "base", "stat", "aggr", "var", "rstd", "x2",
            "turned", "x2hi", "x2lo", "mm", "sum", "tanh", "out", "bo_in")}

        probs_w = probs[:, :, :, :].rearrange("p a h k -> p (a h k)").rearrange("p (k n) -> p k n", k=G)

        e_x_in = [sem(f"e_x_in{t}") for t in range(TT)]
        e_stored = [sem(f"e_stored{t}") for t in range(TT)]

        block = ctx.enter_context(nc.Block())

        def at(eng, s, per, b, k):
            if isinstance(b, int):
                if per * b + k > 0:
                    eng.wait_ge(s, per * b + k)
            else:
                eng.wait_ge(s, b * per + k)
                if eng is nc.sync:
                    unregistered(eng)

        def unregistered(eng):
            eng.sem_inc(passed, 1)

        def bodies(eng, body):
            body(0, attn_kinds, None)
            with eng.Fori(1, B) as b:
                body(b, attn_kinds + cell_kinds, b - 1)
            body(B, cell_kinds, B - 1)

        @block.sync
        def _(sp):
            x_v = x.rearrange("b (t p) (g c) -> b t p g c", p=P, c=P)

            def load_x(b):
                at(sp, projected, TT, b, 0)
                for t in range(TT):
                    sp.dma_start(xa[:, :, t * P:(t + 1) * P], x_v[b, t]).then_inc(x_in, DMA)

            def stack(dst, order, cols, s):
                for r, part in enumerate(order):
                    src = (stage_hi, stage_lo)[part]
                    for h in range(HPG):
                        rows = src[HEAD * h:HEAD * (h + 1), cols]
                        sp.dma_start(dst[HEAD * r:HEAD * (r + 1), h, cols].bitcast(F32),
                                     rows.bitcast(F32) if part == 0 else rows).then_inc(s, DMA)

            def body(b, kinds, _):
                first = isinstance(b, int) and b == 0
                for kind, n in steps:
                    if kind not in kinds:
                        continue
                    if kind == "norm1":
                        load_x(b)
                    if kind == "prep":
                        g = n
                        for landed in q_stacked:
                            at(sp, landed, NSTACK * G, b, NSTACK * g)
                        sp.dma_start(stage_lo[:, :], ctx_t[b, g * P:(g + 1) * P, :]).then_inc(k_in, DMA)
                        at(sp, valued, SLOTS, b, TT * (g - 1))
                        rows = ctx_rows[b].rearrange("(t p) c -> p t c", p=P)
                        sp.dma_start(values[:, g % 2, 0:TT, :],
                                     rows[:, :, g * P:(g + 1) * P]).then_inc(v_in[g % 2], DMA)
                        rows = ctx_rows[b, WINDOW:T - WINDOW, :].rearrange("(t p) c -> p t c", p=P)
                        sp.dma_start(values[:, g % 2, TT:NV, :],
                                     rows[:, :, g * P:(g + 1) * P]).then_inc(v_in[g % 2], DMA)
                        at(sp, k_lo, G, b, g + 1)
                        at(sp, k_hi, G, b, g + 1)
                        at(sp, scored, 2 * SLOTS, b, 2 * TT * (g - 1))
                        stack(key_stack[:, g % 2], (0, 1, 0, 1), slice(0, T), k_stacked)
                        at(sp, q_lo, G, b, g + 1)
                        at(sp, q_hi, G, b, g + 1)
                        for half_ in range(2):
                            at(sp, scored, 2 * SLOTS, b, 2 * (TT * (g - 1) + TT // 2 * (half_ + 1)))
                            stack(query_stack, (0, 0, 1, 1), slice(half_ * T // 2, (half_ + 1) * T // 2), q_stacked[half_])
                        if first and g == 0:
                            load_weights(0, G)
                    if kind == "value" and first and n >= TT:
                        s = n - TT
                        load_weights(WPS * s + G, min(WPS * (s + 1) + G, NCH))
                    if kind == "weights":
                        at(sp, turned, 2 * SLOTS, b, 2 * SLOTS)
                        sp.dma_start(probs_w, w_proj.rearrange("(k p) n -> p k n", p=P)).then_inc(proj_in, DMA)
                    if kind == "proj":
                        t = n
                        at(sp, x1_out[t % 2], DMA * TT // 2, b, DMA * (t // 2))
                        at(sp, x2_done, TT, b, t - 1)
                        sp.dma_start(xr[:, t % 2, :], x[b, t * P:(t + 1) * P, :]).then_inc(xr_in[t % 2], DMA)

            def load_weights(n0, n1):
                for n in range(n0, n1):
                    at(sp, w_lo, 0, 0, n - G + 1)
                    gt, u, k = chunks[n]
                    sp.dma_start(state[:, n % G, :], (u_gates if u else w_gates)[gt][k * P:(k + 1) * P, :])\
                      .then_inc(w_in[n % G], DMA)

            for gt in range(NG):
                sp.dma_start(bias[:, gt, :], biases[gt]).then_inc(const_in, DMA)
            sp.dma_start(c0[:, :], in_c).then_inc(const_in, DMA)
            sp.dma_start(bp_row[:, :], b_proj.partition_broadcast(P)).then_inc(bp_in, DMA)
            bodies(sp, body)

            at(sp, projected, TT, B, 0)
            sp.dma_start(xa[:, :, :], w_out.rearrange("(k p) n -> p k n", p=P)).then_inc(e["raw_in"], DMA)
            sp.dma_start(probs_w, u_out.rearrange("(k p) n -> p k n", p=P)).then_inc(e["raw_in"], DMA)
            at(sp, xr_ready, TT, B, 0)
            sp.dma_start(bp_row[:, :], b_out.partition_broadcast(P)).then_inc(e["bo_in"], DMA)
            for stored in x1_out:
                at(sp, stored, DMA * TT // 2, B, 0)

            def last(b):
                for t in range(TT):
                    if isinstance(b, int) and b == 0:
                        if t == 0:
                            sp.wait_ge(e["lo"], 2 * G)
                    else:
                        at(sp, e_stored[t], DMA, b, 0)
                    sp.dma_start(xa[:, t, :], x1_dram[b, t * P:(t + 1) * P, :]).then_inc(e_x_in[t], DMA)
                    if t >= 2:
                        store(b, t - 2)
                store(b, TT - 2)
                store(b, TT - 1)

            def store(b, t):
                at(sp, e["out"], TT, b, t + 1)
                sp.dma_start(out[b, t * P:(t + 1) * P, :], xa[:, t, :]).then_inc(e_stored[t], DMA)

            last(0)
            with sp.Fori(1, B) as b:
                last(b)
            for stored in e_stored:
                sp.wait_ge(stored, DMA * B)

        @block.gpsimd
        def _(pool):
            pool.memset(ident[:, :], 0.0).then_inc(consts, 1)
            pool.memset(mask[:, :], 0.0).then_inc(consts, 1)
            pool.memset(half[:, :], -0.5).then_inc(consts, 1)
            pool.wait_ge(consts, 3)
            pool.affine_select(out=ident[:, :], in_=ident[:, :], compare_op=ALU.not_equal, fill=1.0,
                               base=0, pattern=[[-1, P]], channel_multiplier=1).then_inc(consts, 1)
            pool.affine_select(out=mask[:, :], in_=mask[:, :], compare_op=ALU.is_ge, fill=NEG,
                               base=-WINDOW, pattern=[[1, MASKW]], channel_multiplier=-1).then_inc(consts, 1)
            pool.wait_ge(consts, 5)
            pool.affine_select(out=mask[:, :], in_=mask[:, :], compare_op=ALU.is_ge, fill=NEG,
                               base=3 * WINDOW, pattern=[[-1, MASKW]], channel_multiplier=1).then_inc(consts, 1)
            pool.wait_ge(bp_in, DMA)

            def body(b, kinds, _):
                if "prep" not in kinds:
                    return
                at(pool, var1, 1, b, 1)
                pool.tensor_tensor(rs1[:, :], ve1[:, :], half[:, :], ALU.pow).then_inc(rstd1, 1)
                for t in range(TT):
                    at(pool, xr_in[t % 2], DMA * TT // 2, b, DMA * (t // 2 + 1))
                    pool.tensor_tensor(xr[:, t % 2, :], xr[:, t % 2, :], bp_row[:, :], ALU.add)\
                        .then_inc(xr_ready, 1)
                    at(pool, var2, TT, b, t + 1)
                    pool.tensor_tensor(rs2[:, :], ve2[:, :], half[:, 0:1], ALU.pow).then_inc(rstd2, 1)
                    at(pool, x1_done, TT, b, t + 1)
                    pool.dma_start(x1_dram[b, t * P:(t + 1) * P, :], xr[:, t % 2, :]).then_inc(x1_out[t % 2], DMA)

            bodies(pool, body)

            def last(b):
                for t in range(TT):
                    at(pool, e["var"], TT, b, t + 1)
                    pool.tensor_tensor(rs2[:, :], ve2[:, :], half[:, 0:1], ALU.pow).then_inc(e["rstd"], 1)
                    if t > 0:
                        total(b, t - 1)
                total(b, TT - 1)

            def total(b, t):
                at(pool, e["tanh"], TT, b, t + 1)
                pool.tensor_tensor(xa[:, t, :], xa[:, t, :], gate[:, t % 2, :], ALU.add).then_inc(e["out"], 1)

            last(0)
            with pool.Fori(1, B) as b:
                last(b)

        @block.tensor
        def _(pe):
            def product(ps, lhs, rhs, start, stop):
                pe.matmul(ps, lhs[0], rhs[0], start=start, stop=False)
                pe.matmul(ps, lhs[0], rhs[1], start=False, stop=False)
                return pe.matmul(ps, lhs[1], rhs[0], start=False, stop=stop)

            pe.wait_ge(consts, 4)

            def body(b, kinds, bc):
                first = isinstance(b, int) and b == 0
                for kind, n in steps:
                    if kind not in kinds:
                        continue
                    if kind == "prep":
                        g = n
                        if g == 0:
                            at(pe, ln1, TT, b, TT)
                            at(pe, x2_lo, TT, b, 0)
                        elif g == 1:
                            at(pe, q_lo, G, b, 1)
                        else:
                            at(pe, recip_out, G, b, g - 1)
                        for t in range(TT):
                            mm = pe.transpose(ps_x[:, t * P:(t + 1) * P], xa[:, g, t * P:(t + 1) * P], ident[:, :])
                        mm.then_inc(q_turned, 1)
                    elif kind == "score":
                        g, t = n // TT, n % TT
                        if t == 0:
                            at(pe, k_stacked, NSTACK * G, b, NSTACK * (g + 1))
                        if t % 2 == 0:
                            at(pe, q_stacked[t // 2], NSTACK * G, b, NSTACK * (g + 1))
                        if n == 0:
                            at(pe, x1_done, TT, b, 0)
                        for h in range(HPG):
                            if h % 2 == 0:
                                at(pe, masked, HPG * SLOTS, b, HPG * n - 2 + h)
                            mm = pe.matmul(ps_s[h // 2][:, (h % 2) * KEYS:(h % 2 + 1) * KEYS],
                                           query_stack[:, h, t * P:(t + 1) * P],
                                           key_stack[:, g % 2, h, KEY0[t]:KEY0[t] + KEYS],
                                           start=True, stop=True)
                            if h % 2 == 1:
                                mm.then_inc(scored, 1)
                    elif kind == "turn":
                        if n == 0:
                            at(pe, x1_done, TT, b, 0)
                        for h in range(HPG):
                            at(pe, expd, HPG * SLOTS, b, HPG * n + h + 1)
                            if h == 0:
                                at(pe, turned_a, SLOTS, b, n)
                            if h == 2:
                                at(pe, turned_b, SLOTS, b, n)
                            for c in range(2):
                                at_ = ((h % 2) * 2 + c) * P
                                mm = pe.transpose(ps_t[h // 2][:, at_:at_ + P],
                                                  probs[:, n % 2, h, c * P:(c + 1) * P], ident[:, :])
                            if h % 2 == 1:
                                mm.then_inc(turned, 1)
                    elif kind == "value":
                        g, t = n // TT, n % TT
                        at(pe, turned_a, SLOTS, b, n + 1)
                        at(pe, turned_b, SLOTS, b, n + 1)
                        if t == 0:
                            at(pe, attn_t, G, b, g)
                            v_count = DMA * G
                            at(pe, v_in[g % 2], v_count, b, DMA * 2 * (g // 2 + 1))
                        for c in range(2):
                            for h in range(HPG):
                                mm = pe.matmul(ps_v[HEAD * h:HEAD * (h + 1), t * P:(t + 1) * P],
                                               values[:, g % 2, VTILES[t][c], HEAD * h:HEAD * (h + 1)],
                                               probs_t[:, 2 * h + c, :], start=(c == 0), stop=(c == 1))
                        mm.then_inc(valued, 1)
                    elif kind == "norm":
                        g = n
                        at(pe, inv, SLOTS, b, TT * (g + 1))
                        if g == 3:
                            at(pe, recip_out, G, b, 3)
                        else:
                            at(pe, q_lo, G, b, g + 2)
                        for t in range(TT):
                            mm = pe.transpose(ps_x[:, t * P:(t + 1) * P],
                                              recip[:, t, :],
                                              ident[:, :])
                        mm.then_inc(spread, 1)
                    elif kind == "proj":
                        t = n
                        if t == 0:
                            at(pe, attn_t, G, b, G)
                            at(pe, proj_in, DMA, b, DMA)
                            at(pe, masked, HPG * SLOTS, b, HPG * SLOTS)
                            at(pe, turned_a, SLOTS, b, SLOTS)
                            at(pe, turned_b, SLOTS, b, SLOTS)
                        for k in range(G):
                            mm = pe.matmul(ps_proj[t][:, :], xa[:, k, t * P:(t + 1) * P], probs_w[:, k, :],
                                           start=(k == 0), stop=(k == G - 1))
                        mm.then_inc(projected, 1)
                    elif kind == "turn2":
                        t = n
                        at(pe, x2_done, TT, b, t + 1)
                        if t == 0:
                            at(pe, recip_out, G, b, G)
                        else:
                            at(pe, x2_lo, TT, b, t)
                        for k in range(G):
                            mm = pe.transpose(ps_x[:, k * P:(k + 1) * P], x2[:, k * P:(k + 1) * P], ident[:, :])
                        mm.then_inc(x2_turned, 1)
                    elif kind == "cell":
                        u, k = n // G, n % G
                        m, gt = u // NG, u % NG
                        if n == 0:
                            if isinstance(bc, int) and bc == 0:
                                pe.wait_ge(w_lo, NCH)
                            at(pe, x2_lo, TT, bc, TT)
                            at(pe, x2_hi, TT, bc, TT)
                            at(pe, c_hi, G, bc, G)
                            at(pe, c_lo, G, bc, G)
                        if k == 0:
                            at(pe, gated, UNITS, bc, max(u - 1, 0))
                        cols = slice(m * P, (m + 1) * P)
                        ps = ps_d[u % 2][:, :]
                        product(ps, (gate_w[:, gt, 0, 0, k, cols], gate_w[:, gt, 0, 1, k, cols]),
                                (x2t_hi[:, k, :], x2t_lo[:, k, :]), k == 0, False)
                        mm = product(ps, (gate_w[:, gt, 1, 0, k, cols], gate_w[:, gt, 1, 1, k, cols]),
                                     (state_hi[:, k, :], state_lo[:, k, :]), False, k == G - 1)
                        if k == G - 1:
                            mm.then_inc(gate_sum, 1)

            bodies(pe, body)

            pe.wait_ge(e["lo"], 2 * G)
            pe.wait_ge(e["hi"], 2 * G)
            at(pe, c_lo, G, B, G)
            for t in range(TT):
                for k in range(G):
                    mm = product(ps_proj[t][:, :], (state_hi[:, k, t * P:(t + 1) * P], state_lo[:, k, t * P:(t + 1) * P]),
                                 (gate_w[:, 0, 1, 0, k, :], gate_w[:, 0, 1, 1, k, :]), k == 0, k == G - 1)
                mm.then_inc(e["base_mm"], 1)

            def last(b):
                def turn(t):
                    at(pe, e["x2"], TT, b, t + 1)
                    at(pe, e["x2lo"], TT, b, t)
                    for k in range(G):
                        mm = pe.transpose(ps_x[:, k * P:(k + 1) * P], x2[:, k * P:(k + 1) * P], ident[:, :])
                    mm.then_inc(e["turned"], 1)

                def mms(t):
                    at(pe, e["x2lo"], TT, b, t + 1)
                    at(pe, e["x2hi"], TT, b, t + 1)
                    at(pe, e["sum"], TT, b, t - 1)
                    for k in range(G):
                        mm = product(ps_d[t % 2][:, :], (x2t_hi[:, k, t * P:(t + 1) * P], x2t_lo[:, k, t * P:(t + 1) * P]),
                                     (gate_w[:, 0, 0, 0, k, :], gate_w[:, 0, 0, 1, k, :]), k == 0, k == G - 1)
                    mm.then_inc(e["mm"], 1)

                turn(0)
                for t in range(TT):
                    if t + 1 < TT:
                        turn(t + 1)
                    mms(t)

            last(0)
            with pe.Fori(1, B) as b:
                last(b)

        @block.scalar
        def _(act):
            def split_weights(n0, n1):
                for n in range(n0, n1):
                    gt, u, k = chunks[n]
                    act.wait_ge(w_in[n % G], DMA * (n // G + 1))
                    act.activation(gate_w[:, gt, u, 0, k, :], state[:, n % G, :], ACT.Copy,
                                   scale=0.5 if u else 1.0).then_inc(w_hi, 1)

            def body(b, kinds, bc):
                first = isinstance(b, int) and b == 0
                for kind, n in steps:
                    if kind not in kinds:
                        continue
                    if kind == "prep":
                        g = n
                        at(act, k_in, DMA * G, b, DMA * (g + 1))
                        act.activation(stage_hi[:, :], stage_lo[:, :], ACT.Copy).then_inc(k_hi, 1)
                        at(act, q_turned, G, b, g + 1)
                        at(act, k_stacked, NSTACK * G, b, NSTACK * (g + 1))
                        act.activation(stage_hi[:, :], ps_x[:, :], ACT.Copy).then_inc(q_hi, 1)
                    elif kind == "score":
                        at(act, nmax, SLOTS, b, n + 1)
                        for h in range(HPG):
                            at(act, inv, SLOTS, b, n - TT + 1)
                            row = probs[:, n % 2, h, :]
                            act.activation(row, row, ACT.Exp, bias=negmax[:, n % 2, h:h + 1], scale=SCALE,
                                           accum_out=rowsum[:, n % TT, h:h + 1]).then_inc(expd, 1)
                    elif kind == "turn":
                        at(act, turned, 2 * SLOTS, b, 2 * n + 1)
                        at(act, valued, SLOTS, b, n)
                        act.activation(probs_t[:, 0:HPG, :], ps_t[0][:, :].rearrange("p (a q) -> p a q", a=HPG),
                                       ACT.Copy).then_inc(turned_a, 1)
                    elif kind == "norm":
                        at(act, spread, G, b, n + 1)
                        at(act, attn_t, G, b, n)
                        at(act, x2_turned, TT, b, 0)
                        act.activation(recip_sb[:, :], ps_x[:, :], ACT.Copy).then_inc(recip_out, 1)
                    elif kind == "turn2":
                        t = n
                        at(act, x2_turned, TT, b, t + 1)
                        if t == 0 and bc is not None:
                            at(act, gate_sum, UNITS, bc, UNITS)
                        act.activation(x2t_hi[:, :, t * P:(t + 1) * P],
                                       ps_x[:, :].rearrange("p (k q) -> p k q", k=G), ACT.Copy).then_inc(x2_hi, 1)
                    elif kind == "cell" and n % G == G - 1:
                        u = n // G
                        m, gt = u // NG, u % NG
                        at(act, gate_sum, UNITS, bc, u + 1)
                        if gt == 2:
                            at(act, in_gate, G, bc, m + 1)
                        else:
                            at(act, cell, G, bc, m)
                        act.activation(gate[:, min(gt, 1), :], ps_d[u % 2][:, :], ACT.Tanh, bias=bias[:, gt, m:m + 1],
                                       scale=1.0 if gt == 0 else 0.5).then_inc(gated, 1)
                    elif kind == "state":
                        for m in range(G):
                            at(act, cell, G, bc, m + 1)
                            at(act, gate_sum, UNITS, bc, UNITS)
                            act.activation(state_hi[:, m, :], state[:, m, :], ACT.Copy).then_inc(c_hi, 1)
                    if first and kind == "value" and n >= TT:
                        split_weights(WPS * (n - TT), WPS * (n - TT + 1))
                if first:
                    for m in range(G):
                        act.wait_ge(c_init, G + m + 1)
                        act.activation(state_hi[:, m, :], state[:, m, :], ACT.Copy).then_inc(c_hi, 1)
                    act.wait_ge(bias_half, 1)

            bodies(act, body)

            at(act, gate_sum, UNITS, B, 0)
            act.wait_ge(e["raw_in"], 2 * DMA)
            for k in range(G):
                act.activation(gate_w[:, 0, 0, 0, k, :], xa[:, k, :], ACT.Copy).then_inc(e["hi"], 1)
            for k in range(G):
                act.activation(gate_w[:, 0, 1, 0, k, :], probs_w[:, k, :], ACT.Copy, scale=0.5).then_inc(e["hi"], 1)

            def last(b):
                for t in range(TT):
                    at(act, e["turned"], TT, b, t + 1)
                    at(act, e["mm"], TT, b, t + 1 - TT)
                    act.activation(x2t_hi[:, :, t * P:(t + 1) * P],
                                   ps_x[:, :].rearrange("p (k q) -> p k q", k=G), ACT.Copy).then_inc(e["x2hi"], 1)
                    if t > 0:
                        tanh(b, t - 1)
                tanh(b, TT - 1)

            def tanh(b, t):
                at(act, e["sum"], TT, b, t + 1)
                act.activation(gate[:, t % 2, :], gate[:, t % 2, :], ACT.Tanh).then_inc(e["tanh"], 1)

            last(0)
            with act.Fori(1, B) as b:
                last(b)

        @block.vector
        def _(dve):
            dve.wait_ge(const_in, DMA * (NG + 1))
            dve.tensor_scalar(bias[:, 1:NG, :], bias[:, 1:NG, :], 0.5, None, ALU.mult).then_inc(bias_half, 1)
            dve.wait_ge(consts, 6)

            def split_weights(n0, n1):
                for n in range(n0, n1):
                    gt, u, k = chunks[n]
                    dve.wait_ge(w_hi, n + 1)
                    dve.scalar_tensor_tensor(out=gate_w[:, gt, u, 1, k, :], in0=state[:, n % G, :],
                                             scalar=0.5 if u else 1.0,
                                             in1=gate_w[:, gt, u, 0, k, :].bitcast(F32),
                                             op0=ALU.mult, op1=ALU.subtract).then_inc(w_lo, 1)

            def body(b, kinds, bc):
                first = isinstance(b, int) and b == 0
                def norm1():
                    for t in range(TT):
                        at(dve, x_in, DMA * TT, b, DMA * TT)
                        dve.bn_stats(st1[:, t, :], xa[:, :, t * P:(t + 1) * P]).then_inc(stat1, 1)
                    for t in range(TT):
                        at(dve, stat1, TT, b, t + 1)
                        unregistered(dve)
                        dve.bn_aggr(mv1[:, t, :], st1[:, t, :]).then_inc(aggr1, 1)
                    at(dve, aggr1, TT, b, TT)
                    dve.tensor_scalar(ve1[:, :], mv1[:, :, 1], EPS, None, ALU.add).then_inc(var1, 1)
                    at(dve, rstd1, 1, b, 1)
                    for t in range(TT):
                        tile = xa[:, :, t * P:(t + 1) * P]
                        dve.tensor_scalar(tile, tile, mv1[:, t, 0:1], rs1[:, t:t + 1], ALU.subtract, ALU.mult)\
                           .then_inc(ln1, 1)
                for kind, n in steps:
                    if kind not in kinds:
                        continue
                    if kind == "norm1":
                        norm1()
                    elif kind == "prep":
                        g = n
                        at(dve, k_hi, G, b, g + 1)
                        dve.tensor_tensor(stage_lo[:, :], stage_lo[:, :], stage_hi[:, :].bitcast(F32),
                                          ALU.subtract).then_inc(k_lo, 1)
                        at(dve, q_hi, G, b, g + 1)
                        dve.tensor_tensor(stage_lo[:, :], ps_x[:, :], stage_hi[:, :].bitcast(F32),
                                          ALU.subtract).then_inc(q_lo, 1)
                    elif kind == "score":
                        g, t = n // TT, n % TT
                        at(dve, turned, 2 * SLOTS, b, 2 * (n - 1))
                        for h in range(HPG):
                            if h % 2 == 0:
                                at(dve, scored, 2 * SLOTS, b, 2 * n + h // 2 + 1)
                                unregistered(dve)
                            dve.tensor_tensor_reduce(probs[:, n % 2, h, :],
                                                     ps_s[h // 2][:, (h % 2) * KEYS:(h % 2 + 1) * KEYS],
                                                     mask[:, MASK0[t]:MASK0[t] + KEYS], 1.0, NEG,
                                                     ALU.add, ALU.max, rowmax[:, n % 2, h:h + 1]).then_inc(masked, 1)
                        at(dve, masked, HPG * SLOTS, b, HPG * (n + 1))
                        dve.tensor_scalar(negmax[:, n % 2, :], rowmax[:, n % 2, :], -SCALE, None, ALU.mult)\
                           .then_inc(nmax, 1)
                    elif kind == "turn":
                        at(dve, turned, 2 * SLOTS, b, 2 * n + 2)
                        at(dve, valued, SLOTS, b, n)
                        dve.tensor_copy(probs_t[:, HPG:2 * HPG, :], ps_t[1][:, :].rearrange("p (a q) -> p a q", a=HPG))\
                           .then_inc(turned_b, 1)
                        at(dve, spread, G, b, n // TT)
                        dve.reciprocal(recip[:, n % TT, :].rearrange("p (h d) -> p h d", h=HPG),
                                       rowsum[:, n % TT, :].unsqueeze(2).to_broadcast([P, HPG, HEAD])).then_inc(inv, 1)
                    elif kind == "norm":
                        at(dve, recip_out, G, b, n + 1)
                        at(dve, valued, SLOTS, b, TT * (n + 1))
                        dve.tensor_tensor(xa[:, n, :], ps_v[:, :], recip_sb[:, :], ALU.mult).then_inc(attn_t, 1)
                    elif kind == "proj":
                        t = n
                        at(dve, projected, TT, b, t + 1)
                        at(dve, xr_ready, TT, b, t + 1)
                        row = xr[:, t % 2, :]
                        dve.tensor_tensor(row, ps_proj[t][:, :], row, ALU.add).then_inc(x1_done, 1)
                        norm2(b, t)
                    elif kind == "turn2":
                        t = n
                        at(dve, x2_hi, TT, b, t + 1)
                        dve.tensor_tensor(x2t_lo[:, :, t * P:(t + 1) * P],
                                          ps_x[:, :].rearrange("p (k q) -> p k q", k=G),
                                          x2t_hi[:, :, t * P:(t + 1) * P].bitcast(F32),
                                          ALU.subtract).then_inc(x2_lo, 1)
                    elif kind == "cell" and n % G == G - 1:
                        u = n // G
                        m, gt = u // NG, u % NG
                        at(dve, gated, UNITS, bc, u + 1)
                        if gt == 1:
                            dve.scalar_tensor_tensor(out=gate[:, 0, :], in0=gate[:, 1, :], scalar=1.0, in1=gate[:, 0, :],
                                                     op0=ALU.add, op1=ALU.mult).then_inc(in_gate, 1)
                        if gt == 2:
                            dve.scalar_tensor_tensor(out=gate[:, 1, :], in0=gate[:, 1, :], scalar=1.0, in1=state[:, m, :],
                                                     op0=ALU.add, op1=ALU.mult).then_inc(kept, 1)
                            at(dve, kept, G, bc, m + 1)
                            at(dve, in_gate, G, bc, m + 1)
                            dve.scalar_tensor_tensor(out=state[:, m, :], in0=gate[:, 1, :], scalar=0.5, in1=gate[:, 0, :],
                                                     op0=ALU.mult, op1=ALU.add).then_inc(cell, 1)
                    elif kind == "state":
                        for m in range(G):
                            at(dve, c_hi, G, bc, G + m + 1)
                            dve.tensor_tensor(state_lo[:, m, :], state[:, m, :], state_hi[:, m, :].bitcast(F32),
                                              ALU.subtract).then_inc(c_lo, 1)
                    if first and kind == "value" and n >= TT:
                        split_weights(WPS * (n - TT), WPS * (n - TT + 1))
                if first:
                    dve.wait_ge(w_lo, NCH)
                    for m in range(G):
                        dve.memset(state[:, m, :], 0.0).then_inc(c_init, 1)
                    dve.wait_ge(c_init, G)
                    for m in range(G):
                        dve.tensor_scalar(state[:, m, :], state[:, m, :], c0[:, m:m + 1], 2.0, ALU.add, ALU.mult)\
                           .then_inc(c_init, 1)
                    for m in range(G):
                        dve.wait_ge(c_hi, m + 1)
                        dve.tensor_tensor(state_lo[:, m, :], state[:, m, :], state_hi[:, m, :].bitcast(F32),
                                          ALU.subtract).then_inc(c_lo, 1)

            def norm2(b, t):
                row = xr[:, t % 2, :]
                at(dve, x1_done, TT, b, t + 1)
                dve.bn_stats(st2[:, :], row).then_inc(stat2, 1)
                at(dve, stat2, TT, b, t + 1)
                unregistered(dve)
                dve.bn_aggr(mv2[:, :], st2[:, :]).then_inc(aggr2, 1)
                at(dve, aggr2, TT, b, t + 1)
                dve.tensor_scalar(ve2[:, :], mv2[:, 1:2], EPS, None, ALU.add).then_inc(var2, 1)
                at(dve, rstd2, TT, b, t + 1)
                at(dve, x2_turned, TT, b, t)
                dve.tensor_scalar(x2[:, :], row, mv2[:, 0:1], rs2[:, 0:1], ALU.subtract, ALU.mult).then_inc(x2_done, 1)

            bodies(dve, body)

            for k in range(G):
                dve.wait_ge(e["hi"], k + 1)
                dve.tensor_tensor(gate_w[:, 0, 0, 1, k, :], xa[:, k, :], gate_w[:, 0, 0, 0, k, :].bitcast(F32),
                                  ALU.subtract).then_inc(e["lo"], 1)
            for k in range(G):
                dve.wait_ge(e["hi"], G + k + 1)
                dve.scalar_tensor_tensor(out=gate_w[:, 0, 1, 1, k, :], in0=probs_w[:, k, :], scalar=0.5,
                                         in1=gate_w[:, 0, 1, 0, k, :].bitcast(F32),
                                         op0=ALU.mult, op1=ALU.subtract).then_inc(e["lo"], 1)
            dve.wait_ge(e["bo_in"], DMA)
            for t in range(TT):
                dve.wait_ge(e["base_mm"], t + 1)
                dve.tensor_tensor(state[:, t, :], ps_proj[t][:, :], bp_row[:, :], ALU.add).then_inc(e["base"], 1)

            def last(b):
                def norm(t):
                    row = xa[:, t, :]
                    at(dve, e_x_in[t], DMA, b, DMA)
                    dve.bn_stats(st2[:, :], row).then_inc(e["stat"], 1)
                    at(dve, e["stat"], TT, b, t + 1)
                    unregistered(dve)
                    dve.bn_aggr(mv2[:, :], st2[:, :]).then_inc(e["aggr"], 1)
                    at(dve, e["aggr"], TT, b, t + 1)
                    dve.tensor_scalar(ve2[:, :], mv2[:, 1:2], EPS, None, ALU.add).then_inc(e["var"], 1)
                    at(dve, e["rstd"], TT, b, t + 1)
                    at(dve, e["turned"], TT, b, t)
                    dve.tensor_scalar(x2[:, :], row, mv2[:, 0:1], rs2[:, 0:1], ALU.subtract, ALU.mult)\
                       .then_inc(e["x2"], 1)

                def low(t):
                    at(dve, e["x2hi"], TT, b, t + 1)
                    dve.tensor_tensor(x2t_lo[:, :, t * P:(t + 1) * P],
                                      ps_x[:, :].rearrange("p (k q) -> p k q", k=G),
                                      x2t_hi[:, :, t * P:(t + 1) * P].bitcast(F32),
                                      ALU.subtract).then_inc(e["x2lo"], 1)

                def total(t):
                    at(dve, e["mm"], TT, b, t + 1)
                    at(dve, e["base"], 0, 0, TT)
                    at(dve, e["out"], TT, b, t - 1)
                    dve.tensor_tensor(gate[:, t % 2, :], ps_d[t % 2][:, :], state[:, t, :], ALU.add)\
                       .then_inc(e["sum"], 1)

                for t in range(TT):
                    norm(t)
                    low(t)
                    if t > 0:
                        total(t - 1)
                total(TT - 1)

            last(0)
            with dve.Fori(1, B) as b:
                last(b)


def kernel(x, ctx_1024, L0_xattn_W_proj, L0_xattn_b_proj, L0_ffn_wf, L0_ffn_uf, L0_ffn_bf, L0_ffn_wi,
           L0_ffn_ui, L0_ffn_bi, L0_ffn_wc, L0_ffn_uc, L0_ffn_bc, L0_ffn_wo, L0_ffn_uo, L0_ffn_bo, L0_ffn_in_c):
    import numpy as np
    import concourse.bacc as bacc
    from concourse.bass_utils import run_bass_kernel_spmd

    def transposed(a):
        return np.ascontiguousarray(np.swapaxes(np.asarray(a), -1, -2))

    def columns(a):
        return np.ascontiguousarray(np.asarray(a).reshape(-1, P).T)

    arrays = {
        "x": np.ascontiguousarray(x), "ctx_rows": np.ascontiguousarray(ctx_1024), "ctx_t": transposed(ctx_1024),
        "w_proj": transposed(L0_xattn_W_proj), "b_proj": np.ascontiguousarray(L0_xattn_b_proj),
        "w_c": transposed(L0_ffn_wc), "w_i": transposed(L0_ffn_wi), "w_f": transposed(L0_ffn_wf),
        "u_c": transposed(L0_ffn_uc), "u_i": transposed(L0_ffn_ui), "u_f": transposed(L0_ffn_uf),
        "b_c": columns(L0_ffn_bc), "b_i": columns(L0_ffn_bi), "b_f": columns(L0_ffn_bf),
        "w_out": transposed(L0_ffn_wo), "u_out": transposed(L0_ffn_uo), "b_out": np.ascontiguousarray(L0_ffn_bo),
        "in_c": columns(L0_ffn_in_c),
    }
    nc = bacc.Bacc("TRN2", target_bir_lowering=False, num_devices=1)
    d = {n: nc.dram_tensor(n, a.shape, mybir.dt.from_np(a.dtype), kind="ExternalInput").ap()
         for n, a in arrays.items()}
    out = nc.dram_tensor("out", arrays["x"].shape, F32, kind="ExternalOutput").ap()
    x1_dram = nc.dram_tensor("x1_dram", arrays["x"].shape, F32, kind="Internal").ap()
    bass_xattn_ffn(nc, d["x"], d["ctx_rows"], d["ctx_t"], d["w_proj"], d["b_proj"],
                   [d["w_c"], d["w_i"], d["w_f"]], [d["u_c"], d["u_i"], d["u_f"]],
                   [d["b_c"], d["b_i"], d["b_f"]], d["w_out"], d["u_out"], d["b_out"], d["in_c"], out, x1_dram)
    r = run_bass_kernel_spmd(nc, [arrays], core_ids=[0])
    return r.results[0]["out"]
```

```python
from contextlib import ExitStack

import concourse.bass as bass
from concourse import mybir

F32 = mybir.dt.float32
F32R = mybir.dt.float32r
ALU = mybir.AluOpType
ACT = mybir.ActivationFunctionType
AX = mybir.AxisListType

P = 128
HEAD = 32
HPG = P // HEAD
WINDOW = 64
KEYS = P + 2 * WINDOW
EPS = 1e-5
NEG = -3.0e38
DMA = 16


def bass_xattn_ffn(nc, x, ctx_rows, ctx_t, w_proj, b_proj, w_gates, u_gates, biases, w_out, u_out,
                   b_out, in_c, out, x1_dram, k_parts, q_parts):
    B, T, D = x.shape
    TT = T // P
    G = D // P
    SCALE = float(HEAD) ** -0.5
    NG = 3
    UNITS = NG * G
    SLOTS = G * TT
    NSTACK = DMA * P // HEAD
    KEY0 = [min(max(P * t - WINDOW, 0), T - KEYS) for t in range(TT)]
    VTILES = [[k // P + c if k % P == 0 else TT + k // P + c for c in range(2)] for k in KEY0]
    NV = 2 * TT - 1
    MASK0 = [WINDOW + KEY0[t] - (P * t - WINDOW) for t in range(TT)]
    MASKW = KEYS + 2 * WINDOW

    AHEAD = 2
    HEADQ, SCOREQ, VALUEQ, TAILQ = (9, 6), 1, 1, 3
    steps = []
    quarters = [(u, h) for u in range(UNITS) for h in range(G) if u >= AHEAD or h >= G // 2]
    q = 0

    def cells(n):
        nonlocal q
        steps.extend(("cell", quarter) for quarter in quarters[q:q + n])
        q += n

    steps.append(("norm1", 0))
    steps.append(("keys", 0))
    cells(HEADQ[0])
    steps.append(("queries", 0))
    cells(HEADQ[1])
    for s in range(SLOTS + 1):
        if s > 0:
            steps.append(("turn", s - 1))
        if s < SLOTS:
            steps.append(("score", s))
            if s % TT == 0 and s // TT + 1 < G:
                steps.append(("keys", s // TT + 1))
            if s % TT == 1 and s // TT + 1 < G:
                steps.append(("queries", s // TT + 1))
        else:
            steps.append(("weights", 0))
        cells(SCOREQ)
        if s > 0:
            steps.append(("value", s - 1))
            if s % TT == 0:
                steps.append(("norm", s // TT - 1))
        left = len(quarters) - q - TAILQ
        if left > SCOREQ * (SLOTS - s):
            cells(min(VALUEQ, left - SCOREQ * (SLOTS - s)))
    cells(len(quarters) - q)
    steps.append(("state", 0))
    for t in range(TT):
        steps.append(("proj", t))
        if t > 0:
            steps.append(("turn2", t - 1))
        steps.append(("norm2", t))
    for u in range(AHEAD):
        steps.append(("ahead", u))
        if u == 0:
            steps.append(("turn2", TT - 1))
    attn_kinds = ("norm1", "keys", "queries", "ahead", "turn", "score", "value", "norm", "weights",
                  "proj", "norm2", "turn2")
    cell_kinds = ("cell", "state")

    chunks = [(g, u, k) for g in range(NG) for u in range(2) for k in range(G)]
    NCH = len(chunks)
    WPS = NCH // (SLOTS - TT)

    with ExitStack() as ctx:
        def sb(name, shape, dt):
            return ctx.enter_context(nc.sbuf_tensor(name, shape, dt))

        def pb(name):
            return ctx.enter_context(nc.psum_tensor(name, [P, 512], F32))

        def sem(name):
            return ctx.enter_context(nc.semaphore(name))

        gate_w = sb("gate_w", [P, NG, 2, 2, G, D], F32R)
        key_stack = sb("key_stack", [P, 2, HPG, T], F32R)
        query_stack = sb("query_stack", [P, HPG, T], F32R)
        x2t_hi = sb("x2t_hi", [P, G, T], F32R)
        x2t_lo = sb("x2t_lo", [P, G, T], F32R)
        xa = sb("xa", [P, G, T], F32)
        state = sb("state", [P, G, T], F32)
        state_hi = sb("state_hi", [P, G, T], F32R)
        state_lo = sb("state_lo", [P, G, T], F32R)
        values = sb("values", [P, 2, NV, P], F32)
        probs = sb("probs", [P, 2, HPG, KEYS], F32)
        probs_t = sb("probs_t", [P, 2 * HPG, P], F32)
        mask = sb("mask", [P, MASKW], F32)
        gate = sb("gate", [P, 2, T], F32)
        stage = sb("stage", [P, 2, T], F32)
        stage_hi = stage[:, 0, :].bitcast(F32R)
        stage_lo = stage[:, 1, :]
        xr = sb("xr", [P, 2, D], F32)
        x2 = sb("x2", [P, D], F32)
        recip_sb = x2[:, :]
        ident = sb("ident", [P, P], F32)
        rowsum = sb("rowsum", [P, TT, HPG], F32)
        recip = sb("recip", [P, TT, P], F32)
        negmax = sb("negmax", [P, 2, HPG], F32)
        rowmax = sb("rowmax", [P, 2, HPG], F32)
        bias = sb("bias", [P, NG, G], F32)
        c0 = sb("c0", [P, G], F32)
        half = sb("half", [P, TT], F32)
        st1 = sb("st1", [P, TT, 6], F32)
        mv1 = sb("mv1", [P, TT, 2], F32)
        ve1 = sb("ve1", [P, TT], F32)
        rs1 = sb("rs1", [P, TT], F32)
        st2 = sb("st2", [P, 6], F32)
        mv2 = sb("mv2", [P, 2], F32)
        ve2 = sb("ve2", [P, 1], F32)
        rs2 = sb("rs2", [P, 1], F32)
        bp_row = sb("bp_row", [P, D], F32)

        ps_s = [pb("ps_s0"), pb("ps_s1")]
        ps_t = [pb("ps_t0"), pb("ps_t1")]
        ps_v = pb("ps_v")
        ps_x = pb("ps_x")
        ps_d = [pb("ps_d0"), pb("ps_d1")]
        ps_proj = ps_s + ps_t
        ps_turn2 = [ps_x, ps_v]

        x_in = [sem(f"x_in{t}") for t in range(TT)]; k_in = sem("k_in"); v_in = [sem("v_in0"), sem("v_in1")]
        k_out = sem("k_out"); q_out = sem("q_out"); k_stacked = sem("k_stacked"); q_stacked = [sem("q_stacked0"), sem("q_stacked1")]
        xr_in = [sem("xr_in0"), sem("xr_in1")]; x1_out = [sem("x1_out0"), sem("x1_out1")]
        w_in = [sem(f"w_in{i}") for i in range(G)]
        const_in = sem("const_in"); proj_in = sem("proj_in"); bp_in = sem("bp_in")
        consts = sem("consts"); rstd1 = sem("rstd1"); rstd2 = sem("rstd2"); xr_ready = sem("xr_ready")
        stat1 = sem("stat1"); aggr1 = sem("aggr1"); var1 = sem("var1"); ln1 = sem("ln1")
        k_lo = sem("k_lo"); q_lo = sem("q_lo"); masked = sem("masked"); nmax = sem("nmax")
        turned_b = sem("turned_b"); inv = sem("inv"); inverted = sem("inverted"); attn_t = sem("attn_t")
        x1_done = sem("x1_done"); stat2 = sem("stat2"); aggr2 = sem("aggr2"); var2 = sem("var2")
        x2_done = sem("x2_done"); x2_lo = sem("x2_lo"); w_lo = sem("w_lo")
        in_gate = sem("in_gate"); kept = sem("kept"); cell = sem("cell"); c_lo = sem("c_lo")
        bias_half = sem("bias_half"); c_init = sem("c_init")
        k_hi = sem("k_hi"); q_hi = sem("q_hi"); expd = sem("expd"); turned_a = sem("turned_a")
        recip_out = sem("recip_out"); x2_hi = sem("x2_hi"); w_hi = sem("w_hi")
        gated = sem("gated"); c_hi = sem("c_hi")
        q_turned = sem("q_turned"); scored = sem("scored"); turned = sem("turned")
        valued = sem("valued"); spread = sem("spread"); projected = sem("projected")
        x2_turned = sem("x2_turned"); gate_sum = sem("gate_sum")
        passed = sem("passed")
        e = {n: sem("e_" + n) for n in (
            "raw_in", "hi", "lo", "base_mm", "base", "stat", "aggr", "var", "rstd", "x2",
            "turned", "x2hi", "x2lo", "mm", "sum", "tanh", "out", "bo_in")}

        def x2_at(t):
            return x2[:, :] if t % 2 == 0 else recip[:, :, :].rearrange("p t c -> p (t c)")

        probs_w = probs[:, :, :, :].rearrange("p a h k -> p (a h k)").rearrange("p (k n) -> p k n", k=G)

        e_x_in = [sem(f"e_x_in{t}") for t in range(TT)]
        e_stored = [sem(f"e_stored{t}") for t in range(TT)]

        block = ctx.enter_context(nc.Block())

        def at(eng, s, per, b, k):
            if isinstance(b, int):
                if per * b + k > 0:
                    eng.wait_ge(s, per * b + k)
            else:
                eng.wait_ge(s, b * per + k)
                if eng is nc.sync:
                    unregistered(eng)

        def unregistered(eng):
            eng.sem_inc(passed, 1)

        def bodies(eng, body):
            body(0, attn_kinds, None)
            body(1, attn_kinds + cell_kinds, 0)
            with eng.Fori(2, B) as b:
                body(b, attn_kinds + cell_kinds, b - 1)
            body(B, cell_kinds, B - 1)

        def exists(b, t):
            return not isinstance(b, int) or 0 <= TT * b + t < TT * B

        def tile_of(b, t):
            return b + t // TT, t % TT

        def tiles(eng, step):
            for t in range(-3, TT):
                step(0, t)
            with eng.Fori(1, B - 1) as b:
                for t in range(TT):
                    step(b, t)
            for t in range(TT + 2):
                step(B - 1, t)

        @block.sync
        def _(sp):
            x_v = x.rearrange("b (t p) (g c) -> b t p g c", p=P, c=P)

            def load_x(b):
                at(sp, projected, TT, b, 0)
                for t in range(TT):
                    sp.dma_start(xa[:, :, t * P:(t + 1) * P], x_v[b, t]).then_inc(x_in[t], DMA)

            def stack(dst, parts, order, cols, s):
                src = parts.rearrange("(h d) s t -> s d h t", h=HPG)
                for r, part in enumerate(order):
                    sp.dma_start(dst[HEAD * r:HEAD * (r + 1), :, cols].bitcast(F32),
                                 src[part, :, :, cols]).then_inc(s, DMA)

            def body(b, kinds, _):
                first = isinstance(b, int) and b == 0
                for kind, n in steps:
                    if kind not in kinds:
                        continue
                    if kind == "norm1":
                        load_x(b)
                    if kind == "keys":
                        g = n
                        at(sp, q_out, DMA * G, b, DMA * g)
                        sp.dma_start(stage_lo, ctx_t[b, g * P:(g + 1) * P, :]).then_inc(k_in, DMA)
                        at(sp, valued, SLOTS, b, TT * (g - 1))
                        rows = ctx_rows[b].rearrange("(t p) c -> p t c", p=P)
                        sp.dma_start(values[:, g % 2, 0:TT, :],
                                     rows[:, :, g * P:(g + 1) * P]).then_inc(v_in[g % 2], DMA)
                        rows = ctx_rows[b, WINDOW:T - WINDOW, :].rearrange("(t p) c -> p t c", p=P)
                        sp.dma_start(values[:, g % 2, TT:NV, :],
                                     rows[:, :, g * P:(g + 1) * P]).then_inc(v_in[g % 2], DMA)
                        at(sp, k_lo, G, b, g + 1)
                        at(sp, k_stacked, NSTACK * G, b, NSTACK * g)
                        sp.dma_start(k_parts, stage[:, :, :]).then_inc(k_out, DMA)
                        at(sp, k_out, DMA * G, b, DMA * (g + 1))
                        at(sp, scored, 2 * SLOTS, b, 2 * TT * (g - 1))
                        stack(key_stack[:, g % 2], k_parts, (0, 1, 0, 1), slice(0, T), k_stacked)
                    if kind == "queries":
                        g = n
                        at(sp, q_lo, G, b, g + 1)
                        for landed in q_stacked:
                            at(sp, landed, NSTACK * G, b, NSTACK * g)
                        sp.dma_start(q_parts, stage[:, :, :]).then_inc(q_out, DMA)
                        at(sp, q_out, DMA * G, b, DMA * (g + 1))
                        for half_ in range(2):
                            at(sp, scored, 2 * SLOTS, b, 2 * (TT * (g - 1) + TT // 2 * (half_ + 1)))
                            stack(query_stack, q_parts, (0, 0, 1, 1), slice(half_ * T // 2, (half_ + 1) * T // 2), q_stacked[half_])
                        if first and g == 0:
                            load_weights(0, G)
                    if kind == "value" and first and n >= TT:
                        s = n - TT
                        load_weights(WPS * s + G, min(WPS * (s + 1) + G, NCH))
                    if kind == "weights":
                        at(sp, turned, 2 * SLOTS, b, 2 * SLOTS)
                        sp.dma_start(probs_w, w_proj.rearrange("(k p) n -> p k n", p=P)).then_inc(proj_in, DMA)
                        load_row(b, 0)
                        load_row(b, 1)
                    if kind == "norm2":
                        at(sp, x1_done, TT, b, n + 1)
                        sp.dma_start(x1_dram[b, n * P:(n + 1) * P, :], xr[:, n % 2, :]).then_inc(x1_out[n % 2], DMA)
                        if n + 2 < TT:
                            load_row(b, n + 2)

            def load_row(b, t):
                at(sp, x1_out[t % 2], DMA * TT // 2, b, DMA * (t // 2))
                at(sp, x2_done, TT, b, t - 1)
                sp.dma_start(xr[:, t % 2, :], x[b, t * P:(t + 1) * P, :]).then_inc(xr_in[t % 2], DMA)

            def load_weights(n0, n1):
                for n in range(n0, n1):
                    at(sp, w_lo, 0, 0, n - G + 1)
                    gt, u, k = chunks[n]
                    sp.dma_start(state[:, n % G, :], (u_gates if u else w_gates)[gt][k * P:(k + 1) * P, :])\
                      .then_inc(w_in[n % G], DMA)

            for gt in range(NG):
                sp.dma_start(bias[:, gt, :], biases[gt]).then_inc(const_in, DMA)
            sp.dma_start(c0[:, :], in_c).then_inc(const_in, DMA)
            sp.dma_start(bp_row[:, :], b_proj.partition_broadcast(P)).then_inc(bp_in, DMA)
            bodies(sp, body)

            at(sp, projected, TT, B, 0)
            sp.dma_start(xa[:, :, :], w_out.rearrange("(k p) n -> p k n", p=P)).then_inc(e["raw_in"], DMA)
            sp.dma_start(probs_w, u_out.rearrange("(k p) n -> p k n", p=P)).then_inc(e["raw_in"], DMA)
            at(sp, xr_ready, TT, B, 0)
            sp.dma_start(bp_row[:, :], b_out.partition_broadcast(P)).then_inc(e["bo_in"], DMA)
            for stored in x1_out:
                at(sp, stored, DMA * TT // 2, B, 0)

            def last(b, t):
                if exists(b, t + 2):
                    at(sp, e["out"], TT, b, t + 2 - TT)
                    at(sp, e["lo"], 0, 0, 2 * G)
                    bt, tt = tile_of(b, t + 2)
                    sp.dma_start(xa[:, tt, :], x1_dram[bt, tt * P:(tt + 1) * P, :]).then_inc(e_x_in[tt], DMA)
                if exists(b, t - 1):
                    at(sp, e["out"], TT, b, t)
                    bt, tt = tile_of(b, t - 1)
                    sp.dma_start(out[bt, tt * P:(tt + 1) * P, :], probs_w[:, tt, :]).then_inc(e_stored[tt], DMA)

            tiles(sp, last)
            for stored in e_stored:
                sp.wait_ge(stored, DMA * B)

        @block.gpsimd
        def _(pool):
            pool.memset(ident[:, :], 0.0).then_inc(consts, 1)
            pool.memset(mask[:, :], 0.0).then_inc(consts, 1)
            pool.memset(half[:, :], -0.5).then_inc(consts, 1)
            pool.wait_ge(consts, 3)
            pool.affine_select(out=ident[:, :], in_=ident[:, :], compare_op=ALU.not_equal, fill=1.0,
                               base=0, pattern=[[-1, P]], channel_multiplier=1).then_inc(consts, 1)
            pool.affine_select(out=mask[:, :], in_=mask[:, :], compare_op=ALU.is_ge, fill=NEG,
                               base=-WINDOW, pattern=[[1, MASKW]], channel_multiplier=-1).then_inc(consts, 1)
            pool.wait_ge(consts, 5)
            pool.affine_select(out=mask[:, :], in_=mask[:, :], compare_op=ALU.is_ge, fill=NEG,
                               base=3 * WINDOW, pattern=[[-1, MASKW]], channel_multiplier=1).then_inc(consts, 1)
            pool.wait_ge(bp_in, DMA)

            def body(b, kinds, _):
                if "proj" not in kinds:
                    return
                at(pool, var1, 1, b, 1)
                pool.tensor_tensor(rs1[:, :], ve1[:, :], half[:, :], ALU.pow).then_inc(rstd1, 1)
                def add_bias(t):
                    at(pool, xr_in[t % 2], DMA * TT // 2, b, DMA * (t // 2 + 1))
                    pool.tensor_tensor(xr[:, t % 2, :], xr[:, t % 2, :], bp_row[:, :], ALU.add)\
                        .then_inc(xr_ready, 1)

                add_bias(0)
                add_bias(1)
                for t in range(TT):
                    at(pool, var2, TT, b, t + 1)
                    pool.tensor_tensor(rs2[:, :], ve2[:, :], half[:, 0:1], ALU.pow).then_inc(rstd2, 1)
                    if t + 2 < TT:
                        add_bias(t + 2)

            bodies(pool, body)

            def last(b, t):
                if exists(b, t + 2):
                    at(pool, e["var"], TT, b, t + 3)
                    pool.tensor_tensor(rs2[:, :], ve2[:, :], half[:, 0:1], ALU.pow).then_inc(e["rstd"], 1)
                if exists(b, t - 1):
                    at(pool, e["tanh"], TT, b, t)
                    tt = (t - 1) % TT
                    pool.tensor_tensor(probs_w[:, tt, :], probs_w[:, tt, :], xa[:, tt, :], ALU.add)\
                        .then_inc(e["out"], 1)

            tiles(pool, last)

        @block.tensor
        def _(pe):
            def product(ps, lhs, rhs, start, stop):
                pe.matmul(ps, lhs[0], rhs[0], start=start, stop=False)
                pe.matmul(ps, lhs[0], rhs[1], start=False, stop=False)
                return pe.matmul(ps, lhs[1], rhs[0], start=False, stop=stop)

            def quarter(u, h):
                m, gt = u // NG, u % NG
                is_u = h < G // 2
                hi, lo = (state_hi, state_lo) if is_u else (x2t_hi, x2t_lo)
                for k in range(G // 2 * (h % 2), G // 2 * (h % 2 + 1)):
                    w = gate_w[:, gt, 1 if is_u else 0, :, k, m * P:(m + 1) * P]
                    mm = product(ps_d[u % 2][:, :], (w[:, 0, :], w[:, 1, :]), (hi[:, k, :], lo[:, k, :]),
                                 h == 0 and k == 0, h == G - 1 and k == G - 1)
                return mm

            pe.wait_ge(consts, 4)

            def body(b, kinds, bc):
                first = isinstance(b, int) and b == 0
                for kind, n in steps:
                    if kind not in kinds:
                        continue
                    if kind == "queries":
                        g = n
                        if g == 0:
                            at(pe, ln1, TT, b, TT)
                            at(pe, x2_lo, TT, b, 0)
                        elif g == 1:
                            at(pe, q_lo, G, b, 1)
                        else:
                            at(pe, recip_out, G, b, g - 1)
                        for t in range(TT):
                            mm = pe.transpose(ps_x[:, t * P:(t + 1) * P], xa[:, g, t * P:(t + 1) * P], ident[:, :])
                        mm.then_inc(q_turned, 1)
                    elif kind == "score":
                        g, t = n // TT, n % TT
                        if t == 0:
                            at(pe, k_stacked, NSTACK * G, b, NSTACK * (g + 1))
                        if t % 2 == 0:
                            at(pe, q_stacked[t // 2], NSTACK * G, b, NSTACK * (g + 1))
                        if n == 0:
                            at(pe, x1_done, TT, b, 0)
                        for h in range(HPG):
                            if h % 2 == 0:
                                at(pe, masked, HPG * SLOTS, b, HPG * n - 2 + h)
                            mm = pe.matmul(ps_s[h // 2][:, (h % 2) * KEYS:(h % 2 + 1) * KEYS],
                                           query_stack[:, h, t * P:(t + 1) * P],
                                           key_stack[:, g % 2, h, KEY0[t]:KEY0[t] + KEYS],
                                           start=True, stop=True)
                            if h % 2 == 1:
                                mm.then_inc(scored, 1)
                    elif kind == "turn":
                        if n == 0:
                            at(pe, x1_done, TT, b, 0)
                        for h in range(HPG):
                            at(pe, expd, HPG * SLOTS, b, HPG * n + h + 1)
                            if h == 0:
                                at(pe, turned_a, SLOTS, b, n)
                            if h == 2:
                                at(pe, turned_b, SLOTS, b, n)
                            for c in range(2):
                                at_ = ((h % 2) * 2 + c) * P
                                mm = pe.transpose(ps_t[h // 2][:, at_:at_ + P],
                                                  probs[:, n % 2, h, c * P:(c + 1) * P], ident[:, :])
                            if h % 2 == 1:
                                mm.then_inc(turned, 1)
                    elif kind == "value":
                        g, t = n // TT, n % TT
                        at(pe, turned_a, SLOTS, b, n + 1)
                        at(pe, turned_b, SLOTS, b, n + 1)
                        if t == 0:
                            at(pe, attn_t, G, b, g)
                            at(pe, x2_lo, TT, b, 0)
                            v_count = DMA * G
                            at(pe, v_in[g % 2], v_count, b, DMA * 2 * (g // 2 + 1))
                        for c in range(2):
                            for h in range(HPG):
                                mm = pe.matmul(ps_v[HEAD * h:HEAD * (h + 1), t * P:(t + 1) * P],
                                               values[:, g % 2, VTILES[t][c], HEAD * h:HEAD * (h + 1)],
                                               probs_t[:, 2 * h + c, :], start=(c == 0), stop=(c == 1))
                        mm.then_inc(valued, 1)
                    elif kind == "norm":
                        g = n
                        at(pe, inv, SLOTS, b, TT * (g + 1))
                        if g == 3:
                            at(pe, recip_out, G, b, 3)
                        else:
                            at(pe, q_lo, G, b, g + 2)
                        for t in range(TT):
                            mm = pe.transpose(ps_x[:, t * P:(t + 1) * P],
                                              recip[:, t, :],
                                              ident[:, :])
                        mm.then_inc(spread, 1)
                    elif kind == "proj":
                        t = n
                        if t == 0:
                            at(pe, attn_t, G, b, G)
                            at(pe, proj_in, DMA, b, DMA)
                            at(pe, masked, HPG * SLOTS, b, HPG * SLOTS)
                            at(pe, turned_a, SLOTS, b, SLOTS)
                            at(pe, turned_b, SLOTS, b, SLOTS)
                        for k in range(G):
                            mm = pe.matmul(ps_proj[t][:, :], xa[:, k, t * P:(t + 1) * P], probs_w[:, k, :],
                                           start=(k == 0), stop=(k == G - 1))
                        mm.then_inc(projected, 1)
                    elif kind == "turn2":
                        t = n
                        at(pe, x2_done, TT, b, t + 1)
                        if t == 0:
                            at(pe, recip_out, G, b, G)
                        if t >= 2:
                            at(pe, x2_lo, TT, b, t - 1)
                        for k in range(G):
                            mm = pe.transpose(ps_turn2[t % 2][:, k * P:(k + 1) * P], x2_at(t)[:, k * P:(k + 1) * P],
                                              ident[:, :])
                        mm.then_inc(x2_turned, 1)
                    elif kind == "ahead":
                        u = n
                        if u == 0:
                            if first:
                                pe.wait_ge(w_lo, NCH)
                            at(pe, c_hi, G, b, G)
                            at(pe, c_lo, G, b, G)
                        if u < 2:
                            at(pe, gated, UNITS, b, 0)
                        for h in range(G // 2):
                            quarter(u, h)
                    elif kind == "cell":
                        u, h = n
                        if n == quarters[0]:
                            at(pe, x2_lo, TT, bc, TT)
                            at(pe, x2_hi, TT, bc, TT)
                        if h == 0:
                            at(pe, gated, UNITS, bc, u - 1)
                        mm = quarter(u, h)
                        if h == G - 1:
                            mm.then_inc(gate_sum, 1)

            bodies(pe, body)

            pe.wait_ge(e["lo"], 2 * G)
            pe.wait_ge(e["hi"], 2 * G)
            at(pe, c_lo, G, B, G)
            for t in range(TT):
                for k in range(G):
                    mm = product(ps_proj[t][:, :], (state_hi[:, k, t * P:(t + 1) * P], state_lo[:, k, t * P:(t + 1) * P]),
                                 (gate_w[:, 0, 1, 0, k, :], gate_w[:, 0, 1, 1, k, :]), k == 0, k == G - 1)
                mm.then_inc(e["base_mm"], 1)

            def last(b, t):
                if exists(b, t + 2):
                    at(pe, e["x2"], TT, b, t + 3)
                    at(pe, e["x2lo"], TT, b, t + 1)
                    for k in range(G):
                        mm = pe.transpose(ps_turn2[t % 2][:, k * P:(k + 1) * P], x2_at(t)[:, k * P:(k + 1) * P],
                                          ident[:, :])
                    mm.then_inc(e["turned"], 1)
                if exists(b, t):
                    tt = t % TT
                    at(pe, e["x2lo"], TT, b, t + 1)
                    at(pe, e["sum"], TT, b, t - 1)
                    for k in range(G):
                        mm = product(ps_d[t % 2][:, :],
                                     (x2t_hi[:, k, tt * P:(tt + 1) * P], x2t_lo[:, k, tt * P:(tt + 1) * P]),
                                     (gate_w[:, 0, 0, 0, k, :], gate_w[:, 0, 0, 1, k, :]), k == 0, k == G - 1)
                    mm.then_inc(e["mm"], 1)

            tiles(pe, last)

        @block.scalar
        def _(act):
            def split_weights(n0, n1):
                for n in range(n0, n1):
                    gt, u, k = chunks[n]
                    act.wait_ge(w_in[n % G], DMA * (n // G + 1))
                    act.activation(gate_w[:, gt, u, 0, k, :], state[:, n % G, :], ACT.Copy,
                                   scale=0.5 if u else 1.0).then_inc(w_hi, 1)

            def body(b, kinds, bc):
                first = isinstance(b, int) and b == 0
                for kind, n in steps:
                    if kind not in kinds:
                        continue
                    if kind == "keys":
                        g = n
                        at(act, k_in, DMA * G, b, DMA * (g + 1))
                        act.activation(stage_hi, stage_lo, ACT.Copy).then_inc(k_hi, 1)
                    elif kind == "queries":
                        g = n
                        at(act, q_turned, G, b, g + 1)
                        at(act, k_out, DMA * G, b, DMA * (g + 1))
                        act.activation(stage_hi, ps_x[:, :], ACT.Copy).then_inc(q_hi, 1)
                    elif kind == "score":
                        at(act, nmax, SLOTS, b, n + 1)
                        for h in range(HPG):
                            at(act, inv, SLOTS, b, n - TT + 1)
                            row = probs[:, n % 2, h, :]
                            act.activation(row, row, ACT.Exp, bias=negmax[:, n % 2, h:h + 1], scale=SCALE,
                                           accum_out=rowsum[:, n % TT, h:h + 1]).then_inc(expd, 1)
                    elif kind == "turn":
                        at(act, turned, 2 * SLOTS, b, 2 * n + 1)
                        at(act, valued, SLOTS, b, n)
                        act.activation(probs_t[:, 0:HPG, :], ps_t[0][:, :].rearrange("p (a q) -> p a q", a=HPG),
                                       ACT.Copy).then_inc(turned_a, 1)
                    elif kind == "norm":
                        at(act, spread, G, b, n + 1)
                        at(act, attn_t, G, b, n)
                        at(act, x2_turned, TT, b, 0)
                        act.activation(recip_sb, ps_x[:, :], ACT.Copy).then_inc(recip_out, 1)
                    elif kind == "turn2":
                        t = n
                        at(act, x2_turned, TT, b, t + 1)
                        if t == 0 and bc is not None:
                            at(act, gate_sum, UNITS, bc, UNITS)
                        act.activation(x2t_hi[:, :, t * P:(t + 1) * P],
                                       ps_turn2[t % 2][:, :].rearrange("p (k q) -> p k q", k=G),
                                       ACT.Copy).then_inc(x2_hi, 1)
                    elif kind == "cell" and n[1] == G - 1:
                        u = n[0]
                        m, gt = u // NG, u % NG
                        at(act, gate_sum, UNITS, bc, u + 1)
                        if gt == 2:
                            at(act, in_gate, G, bc, m + 1)
                        else:
                            at(act, cell, G, bc, m)
                        act.activation(gate[:, min(gt, 1), :], ps_d[u % 2][:, :], ACT.Tanh, bias=bias[:, gt, m:m + 1],
                                       scale=1.0 if gt == 0 else 0.5).then_inc(gated, 1)
                    elif kind == "state":
                        for m in range(G):
                            at(act, cell, G, bc, m + 1)
                            at(act, gate_sum, UNITS, bc, UNITS)
                            act.activation(state_hi[:, m, :], state[:, m, :], ACT.Copy).then_inc(c_hi, 1)
                    if first and kind == "value" and n >= TT:
                        split_weights(WPS * (n - TT), WPS * (n - TT + 1))
                    if first and kind == "ahead" and n == 0:
                        for m in range(G):
                            act.wait_ge(c_init, G + m + 1)
                            act.activation(state_hi[:, m, :], state[:, m, :], ACT.Copy).then_inc(c_hi, 1)
                        act.wait_ge(bias_half, 1)

            bodies(act, body)

            at(act, gate_sum, UNITS, B, 0)
            act.wait_ge(e["raw_in"], 2 * DMA)
            for k in range(G):
                act.activation(gate_w[:, 0, 0, 0, k, :], xa[:, k, :], ACT.Copy).then_inc(e["hi"], 1)
            for k in range(G):
                act.activation(gate_w[:, 0, 1, 0, k, :], probs_w[:, k, :], ACT.Copy, scale=0.5).then_inc(e["hi"], 1)

            def last(b, t):
                if exists(b, t + 2):
                    tt = (t + 2) % TT
                    at(act, e["turned"], TT, b, t + 3)
                    at(act, e["mm"], TT, b, t - 1)
                    act.activation(x2t_hi[:, :, tt * P:(tt + 1) * P],
                                   ps_turn2[t % 2][:, :].rearrange("p (k q) -> p k q", k=G),
                                   ACT.Copy).then_inc(e["x2hi"], 1)
                if exists(b, t - 1):
                    row = probs_w[:, (t - 1) % TT, :]
                    at(act, e["sum"], TT, b, t)
                    act.activation(row, row, ACT.Tanh).then_inc(e["tanh"], 1)

            tiles(act, last)

        @block.vector
        def _(dve):
            dve.wait_ge(const_in, DMA * (NG + 1))
            dve.tensor_scalar(bias[:, 1:NG, :], bias[:, 1:NG, :], 0.5, None, ALU.mult).then_inc(bias_half, 1)
            dve.wait_ge(consts, 6)

            def split_weights(n0, n1):
                for n in range(n0, n1):
                    gt, u, k = chunks[n]
                    dve.wait_ge(w_hi, n + 1)
                    dve.scalar_tensor_tensor(out=gate_w[:, gt, u, 1, k, :], in0=state[:, n % G, :],
                                             scalar=0.5 if u else 1.0,
                                             in1=gate_w[:, gt, u, 0, k, :].bitcast(F32),
                                             op0=ALU.mult, op1=ALU.subtract).then_inc(w_lo, 1)

            def body(b, kinds, bc):
                first = isinstance(b, int) and b == 0
                def norm1():
                    for t in range(TT):
                        at(dve, x_in[t], DMA, b, DMA)
                        dve.bn_stats(st1[:, t, :], xa[:, :, t * P:(t + 1) * P]).then_inc(stat1, 1)
                    for t in range(TT):
                        at(dve, stat1, TT, b, t + 1)
                        unregistered(dve)
                        dve.bn_aggr(mv1[:, t, :], st1[:, t, :]).then_inc(aggr1, 1)
                    at(dve, aggr1, TT, b, TT)
                    dve.tensor_scalar(ve1[:, :], mv1[:, :, 1], EPS, None, ALU.add).then_inc(var1, 1)
                    at(dve, rstd1, 1, b, 1)
                    for t in range(TT):
                        tile = xa[:, :, t * P:(t + 1) * P]
                        dve.tensor_scalar(tile, tile, mv1[:, t, 0:1], rs1[:, t:t + 1], ALU.subtract, ALU.mult)\
                           .then_inc(ln1, 1)
                for kind, n in steps:
                    if kind not in kinds:
                        continue
                    if kind == "norm1":
                        norm1()
                    elif kind == "keys":
                        g = n
                        at(dve, k_hi, G, b, g + 1)
                        dve.tensor_tensor(stage_lo, stage_lo, stage[:, 0, :],
                                          ALU.subtract).then_inc(k_lo, 1)
                    elif kind == "queries":
                        g = n
                        at(dve, q_hi, G, b, g + 1)
                        dve.tensor_tensor(stage_lo, ps_x[:, :], stage[:, 0, :],
                                          ALU.subtract).then_inc(q_lo, 1)
                    elif kind == "score":
                        g, t = n // TT, n % TT
                        at(dve, turned, 2 * SLOTS, b, 2 * (n - 1))
                        for h in range(HPG):
                            if h % 2 == 0:
                                at(dve, scored, 2 * SLOTS, b, 2 * n + h // 2 + 1)
                                unregistered(dve)
                            dve.tensor_tensor_reduce(probs[:, n % 2, h, :],
                                                     ps_s[h // 2][:, (h % 2) * KEYS:(h % 2 + 1) * KEYS],
                                                     mask[:, MASK0[t]:MASK0[t] + KEYS], 1.0, NEG,
                                                     ALU.add, ALU.max, rowmax[:, n % 2, h:h + 1]).then_inc(masked, 1)
                        at(dve, masked, HPG * SLOTS, b, HPG * (n + 1))
                        dve.tensor_scalar(negmax[:, n % 2, :], rowmax[:, n % 2, :], -SCALE, None, ALU.mult)\
                           .then_inc(nmax, 1)
                    elif kind == "turn":
                        at(dve, turned, 2 * SLOTS, b, 2 * n + 2)
                        at(dve, valued, SLOTS, b, n)
                        dve.tensor_copy(probs_t[:, HPG:2 * HPG, :], ps_t[1][:, :].rearrange("p (a q) -> p a q", a=HPG))\
                           .then_inc(turned_b, 1)
                        at(dve, spread, G, b, n // TT)
                        at(dve, x2_turned, TT, b, 0)
                        dve.reciprocal(rowsum[:, n % TT, :], rowsum[:, n % TT, :]).then_inc(inverted, 1)
                        at(dve, inverted, SLOTS, b, n + 1)
                        dve.tensor_copy(recip[:, n % TT, :].rearrange("p (h d) -> p h d", h=HPG),
                                        rowsum[:, n % TT, :].unsqueeze(2).to_broadcast([P, HPG, HEAD])).then_inc(inv, 1)
                    elif kind == "norm":
                        at(dve, recip_out, G, b, n + 1)
                        at(dve, valued, SLOTS, b, TT * (n + 1))
                        dve.tensor_tensor(xa[:, n, :], ps_v[:, :], recip_sb, ALU.mult).then_inc(attn_t, 1)
                    elif kind == "proj":
                        t = n
                        at(dve, projected, TT, b, t + 1)
                        at(dve, xr_ready, TT, b, t + 1)
                        row = xr[:, t % 2, :]
                        dve.tensor_tensor(row, ps_proj[t][:, :], row, ALU.add).then_inc(x1_done, 1)
                        stats2(b, t)
                    elif kind == "norm2":
                        norm2(b, n)
                    elif kind == "turn2":
                        t = n
                        at(dve, x2_hi, TT, b, t + 1)
                        dve.tensor_tensor(x2t_lo[:, :, t * P:(t + 1) * P],
                                          ps_turn2[t % 2][:, :].rearrange("p (k q) -> p k q", k=G),
                                          x2t_hi[:, :, t * P:(t + 1) * P].bitcast(F32),
                                          ALU.subtract).then_inc(x2_lo, 1)
                    elif kind == "cell" and n[1] == G - 1:
                        u = n[0]
                        m, gt = u // NG, u % NG
                        at(dve, gated, UNITS, bc, u + 1)
                        if gt == 1:
                            dve.scalar_tensor_tensor(out=gate[:, 0, :], in0=gate[:, 1, :], scalar=1.0, in1=gate[:, 0, :],
                                                     op0=ALU.add, op1=ALU.mult).then_inc(in_gate, 1)
                        if gt == 2:
                            dve.scalar_tensor_tensor(out=gate[:, 1, :], in0=gate[:, 1, :], scalar=1.0, in1=state[:, m, :],
                                                     op0=ALU.add, op1=ALU.mult).then_inc(kept, 1)
                            at(dve, kept, G, bc, m + 1)
                            at(dve, in_gate, G, bc, m + 1)
                            dve.scalar_tensor_tensor(out=state[:, m, :], in0=gate[:, 1, :], scalar=0.5, in1=gate[:, 0, :],
                                                     op0=ALU.mult, op1=ALU.add).then_inc(cell, 1)
                    elif kind == "state":
                        for m in range(G):
                            at(dve, c_hi, G, bc, G + m + 1)
                            dve.tensor_tensor(state_lo[:, m, :], state[:, m, :], state_hi[:, m, :].bitcast(F32),
                                              ALU.subtract).then_inc(c_lo, 1)
                    if first and kind == "value" and n >= TT:
                        split_weights(WPS * (n - TT), WPS * (n - TT + 1))
                    if first and kind == "ahead" and n == 0:
                        dve.wait_ge(w_lo, NCH)
                        for m in range(G):
                            dve.memset(state[:, m, :], 0.0).then_inc(c_init, 1)
                        dve.wait_ge(c_init, G)
                        for m in range(G):
                            dve.tensor_scalar(state[:, m, :], state[:, m, :], c0[:, m:m + 1], 2.0, ALU.add, ALU.mult)\
                               .then_inc(c_init, 1)
                        for m in range(G):
                            dve.wait_ge(c_hi, m + 1)
                            dve.tensor_tensor(state_lo[:, m, :], state[:, m, :], state_hi[:, m, :].bitcast(F32),
                                              ALU.subtract).then_inc(c_lo, 1)

            def stats2(b, t):
                row = xr[:, t % 2, :]
                at(dve, x1_done, TT, b, t + 1)
                dve.bn_stats(st2[:, :], row).then_inc(stat2, 1)
                at(dve, stat2, TT, b, t + 1)
                unregistered(dve)
                dve.bn_aggr(mv2[:, :], st2[:, :]).then_inc(aggr2, 1)
                at(dve, aggr2, TT, b, t + 1)
                dve.tensor_scalar(ve2[:, :], mv2[:, 1:2], EPS, None, ALU.add).then_inc(var2, 1)

            def norm2(b, t):
                row = xr[:, t % 2, :]
                at(dve, rstd2, TT, b, t + 1)
                at(dve, x2_turned, TT, b, t - 1)
                dve.tensor_scalar(x2_at(t), row, mv2[:, 0:1], rs2[:, 0:1], ALU.subtract, ALU.mult).then_inc(x2_done, 1)

            bodies(dve, body)

            for k in range(G):
                dve.wait_ge(e["hi"], k + 1)
                dve.tensor_tensor(gate_w[:, 0, 0, 1, k, :], xa[:, k, :], gate_w[:, 0, 0, 0, k, :].bitcast(F32),
                                  ALU.subtract).then_inc(e["lo"], 1)
            for k in range(G):
                dve.wait_ge(e["hi"], G + k + 1)
                dve.scalar_tensor_tensor(out=gate_w[:, 0, 1, 1, k, :], in0=probs_w[:, k, :], scalar=0.5,
                                         in1=gate_w[:, 0, 1, 0, k, :].bitcast(F32),
                                         op0=ALU.mult, op1=ALU.subtract).then_inc(e["lo"], 1)
            dve.wait_ge(e["bo_in"], DMA)
            for t in range(TT):
                dve.wait_ge(e["base_mm"], t + 1)
                dve.tensor_tensor(state[:, t, :], ps_proj[t][:, :], bp_row[:, :], ALU.add).then_inc(e["base"], 1)

            def last(b, t):
                if exists(b, t + 2):
                    row = xa[:, (t + 2) % TT, :]
                    bt, tt = tile_of(b, t + 2)
                    at(dve, e_x_in[tt], DMA, bt, DMA)
                    dve.bn_stats(st2[:, :], row).then_inc(e["stat"], 1)
                    at(dve, e["stat"], TT, b, t + 3)
                    unregistered(dve)
                    dve.bn_aggr(mv2[:, :], st2[:, :]).then_inc(e["aggr"], 1)
                    at(dve, e["aggr"], TT, b, t + 3)
                    dve.tensor_scalar(ve2[:, :], mv2[:, 1:2], EPS, None, ALU.add).then_inc(e["var"], 1)
                if exists(b, t - 1):
                    tt = (t - 1) % TT
                    at(dve, e["mm"], TT, b, t)
                    at(dve, e["base"], 0, 0, TT)
                    bt, _ = tile_of(b, t - 1)
                    at(dve, e_stored[tt], DMA, bt, 0)
                    dve.tensor_tensor(probs_w[:, tt, :], ps_d[(t - 1) % 2][:, :], state[:, tt, :], ALU.add)\
                       .then_inc(e["sum"], 1)
                if exists(b, t + 1):
                    tt = (t + 1) % TT
                    at(dve, e["x2hi"], TT, b, t + 2)
                    dve.tensor_tensor(x2t_lo[:, :, tt * P:(tt + 1) * P],
                                      ps_turn2[(t + 1) % 2][:, :].rearrange("p (k q) -> p k q", k=G),
                                      x2t_hi[:, :, tt * P:(tt + 1) * P].bitcast(F32),
                                      ALU.subtract).then_inc(e["x2lo"], 1)
                if exists(b, t + 2):
                    at(dve, e["rstd"], TT, b, t + 3)
                    at(dve, e["turned"], TT, b, t + 1)
                    dve.tensor_scalar(x2_at(t), row, mv2[:, 0:1], rs2[:, 0:1], ALU.subtract, ALU.mult)\
                       .then_inc(e["x2"], 1)

            tiles(dve, last)


def kernel(x, ctx_1024, L0_xattn_W_proj, L0_xattn_b_proj, L0_ffn_wf, L0_ffn_uf, L0_ffn_bf, L0_ffn_wi,
           L0_ffn_ui, L0_ffn_bi, L0_ffn_wc, L0_ffn_uc, L0_ffn_bc, L0_ffn_wo, L0_ffn_uo, L0_ffn_bo, L0_ffn_in_c):
    import numpy as np
    import concourse.bacc as bacc
    from concourse.bass_utils import run_bass_kernel_spmd

    def transposed(a):
        return np.ascontiguousarray(np.swapaxes(np.asarray(a), -1, -2))

    def columns(a):
        return np.ascontiguousarray(np.asarray(a).reshape(-1, P).T)

    arrays = {
        "x": np.ascontiguousarray(x), "ctx_rows": np.ascontiguousarray(ctx_1024), "ctx_t": transposed(ctx_1024),
        "w_proj": transposed(L0_xattn_W_proj), "b_proj": np.ascontiguousarray(L0_xattn_b_proj),
        "w_c": transposed(L0_ffn_wc), "w_i": transposed(L0_ffn_wi), "w_f": transposed(L0_ffn_wf),
        "u_c": transposed(L0_ffn_uc), "u_i": transposed(L0_ffn_ui), "u_f": transposed(L0_ffn_uf),
        "b_c": columns(L0_ffn_bc), "b_i": columns(L0_ffn_bi), "b_f": columns(L0_ffn_bf),
        "w_out": transposed(L0_ffn_wo), "u_out": transposed(L0_ffn_uo), "b_out": np.ascontiguousarray(L0_ffn_bo),
        "in_c": columns(L0_ffn_in_c),
    }
    nc = bacc.Bacc("TRN2", target_bir_lowering=False, num_devices=1)
    d = {n: nc.dram_tensor(n, a.shape, mybir.dt.from_np(a.dtype), kind="ExternalInput").ap()
         for n, a in arrays.items()}
    out = nc.dram_tensor("out", arrays["x"].shape, F32, kind="ExternalOutput").ap()
    x1_dram = nc.dram_tensor("x1_dram", arrays["x"].shape, F32, kind="Internal").ap()
    k_parts, q_parts = (nc.dram_tensor(n, (P, 2, arrays["x"].shape[1]), F32, kind="Internal").ap()
                        for n in ("k_parts", "q_parts"))
    bass_xattn_ffn(nc, d["x"], d["ctx_rows"], d["ctx_t"], d["w_proj"], d["b_proj"],
                   [d["w_c"], d["w_i"], d["w_f"]], [d["u_c"], d["u_i"], d["u_f"]],
                   [d["b_c"], d["b_i"], d["b_f"]], d["w_out"], d["u_out"], d["b_out"], d["in_c"], out, x1_dram,
                   k_parts, q_parts)
    r = run_bass_kernel_spmd(nc, [arrays], core_ids=[0])
    return r.results[0]["out"]
```

```python
from contextlib import ExitStack

import concourse.bass as bass
from concourse import mybir

F32 = mybir.dt.float32
F32R = mybir.dt.float32r
ALU = mybir.AluOpType
ACT = mybir.ActivationFunctionType

P = 128
HEAD = 32
HPG = P // HEAD
WINDOW = 64
KEYS = P + 2 * WINDOW
EPS = 1e-5
NEG = -3.0e38
DMA = 16


def bass_xattn_ffn(nc, x, x_by_d, ctx_rows, ctx_t, w_proj, b_proj, w_gates, u_gates, biases, w_out, u_out,
                   b_out, in_c, out, x1_dram, k_parts, q_parts):
    B, T, D = x.shape
    TT = T // P
    G = D // P
    SCALE = float(HEAD) ** -0.5
    NG = 3
    UNITS = NG * G
    SLOTS = G * TT
    NSTACK = 2 * DMA
    KEY0 = [min(max(P * t - WINDOW, 0), T - KEYS) for t in range(TT)]
    VTILES = [[k // P + c if k % P == 0 else TT + k // P + c for c in range(2)] for k in KEY0]
    NV = 2 * TT - 1
    MASK0 = [WINDOW + KEY0[t] - (P * t - WINDOW) for t in range(TT)]
    MASKW = KEYS + 2 * WINDOW

    AHEAD = 2
    HEADQ, PROJQ = (9, 7, 1), (1, 1, 2)
    steps = []
    quarters = [(u, h) for u in range(UNITS) for h in range(G) if u >= AHEAD or h >= G // 2]
    q = 0

    def cells(n):
        nonlocal q
        for quarter in quarters[q:q + n]:
            steps.append(("cell", quarter))
            if q > 0 and quarters[q - 1][1] == G - 1:
                steps.append(("gate", quarters[q - 1][0]))
            q += 1

    def spread_cells(i):
        spare = len(quarters) - sum(HEADQ) - sum(PROJQ)
        cells(spare * (i + 1) // (2 * SLOTS + 2) - spare * i // (2 * SLOTS + 2))

    steps.append(("norm1", 0))
    steps.append(("keys", 0))
    cells(HEADQ[0])
    steps.append(("queries", 0))
    cells(HEADQ[1])
    steps.append(("keys", 1))
    steps.append(("score", 0))
    cells(HEADQ[2])
    for s in range(SLOTS + 1):
        if s > 0:
            steps.append(("turn", s - 1))
        if s < SLOTS and s % TT == 1 and s // TT + 1 < G:
            steps.append(("queries", s // TT + 1))
        if s < SLOTS:
            steps.append(("exp", s))
            if s % TT == TT - 1 and s // TT + 2 < G:
                steps.append(("keys", s // TT + 2))
        else:
            steps.append(("weights", 0))
        spread_cells(2 * s)
        if s + 1 < SLOTS:
            steps.append(("score", s + 1))
        if s > 0:
            steps.append(("value", s - 1))
            if s % TT == 0:
                steps.append(("norm", s // TT - 1))
        spread_cells(2 * s + 1)
    ahead = [("ahead", (u, h)) for u in range(AHEAD) for h in range(G // 2)]
    cells(PROJQ[0])
    for t in range(TT):
        steps.append(("proj", t))
        if t < 2:
            cells(PROJQ[t + 1])
        if t == 1:
            steps.append(("gate", UNITS - 1))
            steps.append(("state", 0))
        if t >= TT - 2:
            steps.append(ahead[t - (TT - 2)])
        if t > 0:
            steps.append(("turn2", t - 1))
        if t == TT - 1:
            steps.append(ahead[2])
        steps.append(("norm2", t))
    steps.append(("turn2", TT - 1))
    steps.extend(ahead[3:])
    attn_kinds = ("norm1", "keys", "queries", "ahead", "turn", "score", "exp", "value", "norm", "weights",
                  "proj", "norm2", "turn2")
    cell_kinds = ("cell", "gate", "state")

    chunks = [(g, u, k) for g in range(NG) for u in range(2) for k in range(G)]
    NCH = len(chunks)
    WPS = NCH // (SLOTS - TT)

    with ExitStack() as ctx:
        def sb(name, shape, dt):
            return ctx.enter_context(nc.sbuf_tensor(name, shape, dt))

        def pb(name):
            return ctx.enter_context(nc.psum_tensor(name, [P, 512], F32))

        def sem(name):
            return ctx.enter_context(nc.semaphore(name))

        gate_w = sb("gate_w", [P, NG, 2, 2, G, D], F32R)
        key_stack = sb("key_stack", [P, 2, HPG, T], F32R)
        query_stack = sb("query_stack", [P, HPG, T], F32R)
        x2t_hi = sb("x2t_hi", [P, G, T], F32R)
        x2t_lo = sb("x2t_lo", [P, G, T], F32R)
        xa = sb("xa", [P, G, T], F32)
        state = sb("state", [P, G, T], F32)
        state_hi = sb("state_hi", [P, G, T], F32R)
        state_lo = sb("state_lo", [P, G, T], F32R)
        values = sb("values", [P, 2, NV, P], F32)
        probs = sb("probs", [P, 2, HPG, KEYS], F32)
        probs_t = sb("probs_t", [P, 2 * HPG, P], F32)
        mask = sb("mask", [P, MASKW], F32)
        gate = sb("gate", [P, 2, T], F32)
        stage = sb("stage", [P, 2, T], F32)
        stage_hi = stage[:, 0, :].bitcast(F32R)
        stage_lo = stage[:, 1, :]
        xr = sb("xr", [P, 2, D], F32)
        x2 = sb("x2", [P, D], F32)
        recip_sb = x2[:, :]
        ident = sb("ident", [P, P], F32)
        rowsum = sb("rowsum", [P, TT, HPG], F32)
        recip = sb("recip", [P, TT, P], F32)
        negmax = sb("negmax", [P, 2, HPG], F32)
        rowmax = sb("rowmax", [P, 2, HPG], F32)
        bias = sb("bias", [P, NG, G], F32)
        c0 = sb("c0", [P, G], F32)
        half = sb("half", [P, TT], F32)
        st1 = sb("st1", [P, TT, 6], F32)
        mv1 = sb("mv1", [P, TT, 2], F32)
        ve1 = sb("ve1", [P, TT], F32)
        rs1 = sb("rs1", [P, TT], F32)
        st2 = sb("st2", [P, 6], F32)
        mv2 = sb("mv2", [P, 2], F32)
        ve2 = sb("ve2", [P, 1], F32)
        rs2 = sb("rs2", [P, 1], F32)
        bp_row = sb("bp_row", [P, D], F32)

        ps_s = [pb("ps_s0"), pb("ps_s1")]
        ps_t = [pb("ps_t0"), pb("ps_t1")]
        ps_v = pb("ps_v")
        ps_x = pb("ps_x")
        ps_d = [pb("ps_d0"), pb("ps_d1")]
        ps_proj = ps_s + ps_t
        ps_turn2 = [ps_x, ps_v]

        x_in = [sem(f"x_in{t}") for t in range(TT)]; k_in = sem("k_in"); v_in = [sem("v_in0"), sem("v_in1")]
        k_out = sem("k_out"); q_out = [sem("q_out0"), sem("q_out1")]; k_stacked = sem("k_stacked"); q_stacked = [sem("q_stacked0"), sem("q_stacked1")]
        xr_in = [sem("xr_in0"), sem("xr_in1")]; x1_out = [sem("x1_out0"), sem("x1_out1")]
        w_in = [sem(f"w_in{i}") for i in range(G)]
        const_in = sem("const_in"); proj_in = sem("proj_in"); bp_in = sem("bp_in")
        consts = sem("consts"); rstd1 = sem("rstd1"); rstd2 = sem("rstd2"); xr_ready = sem("xr_ready")
        stat1 = sem("stat1"); aggr1 = sem("aggr1"); var1 = sem("var1"); ln1 = sem("ln1")
        k_lo = sem("k_lo"); q_lo = sem("q_lo"); masked = sem("masked"); nmax = sem("nmax")
        turned_b = sem("turned_b"); inv = sem("inv"); inverted = sem("inverted"); attn_t = sem("attn_t")
        x1_done = sem("x1_done"); stat2 = sem("stat2"); aggr2 = sem("aggr2"); var2 = sem("var2")
        x2_done = sem("x2_done"); x2_lo = sem("x2_lo"); w_lo = sem("w_lo")
        in_gate = sem("in_gate"); kept = sem("kept"); cell = sem("cell"); c_lo = sem("c_lo")
        bias_half = sem("bias_half"); c_init = sem("c_init")
        k_hi = sem("k_hi"); q_hi = sem("q_hi"); expd = sem("expd"); turned_a = sem("turned_a")
        recip_out = sem("recip_out"); x2_hi = sem("x2_hi"); w_hi = sem("w_hi")
        gated = sem("gated"); c_hi = sem("c_hi")
        q_turned = sem("q_turned"); scored = sem("scored"); turned = sem("turned")
        valued = sem("valued"); spread = sem("spread"); projected = sem("projected")
        x2_turned = sem("x2_turned"); gate_sum = sem("gate_sum")
        passed = sem("passed")
        e = {n: sem("e_" + n) for n in (
            "raw_in", "hi", "lo", "base_mm", "base", "stat", "aggr", "var", "rstd", "x2",
            "turned", "x2hi", "x2lo", "mm", "sum", "tanh", "out", "bo_in")}

        def x2_at(t):
            return x2[:, :] if t % 2 == 0 else recip[:, :, :].rearrange("p t c -> p (t c)")

        probs_w = probs[:, :, :, :].rearrange("p a h k -> p (a h k)").rearrange("p (k n) -> p k n", k=G)

        RING = 2 * TT
        AHEAD_X1 = 5
        wo_hi, wo_lo, uo_hi, uo_lo = key_stack[:, 0], key_stack[:, 1], query_stack, gate_w[:, 0, 1, 1]
        wo_raw, uo_raw = xa, probs_w
        x1_ring = gate_w[:, 1].rearrange("p u s k n -> p (u s k n)").rearrange("p (r n) -> p r n", n=D).bitcast(F32)
        h_ring = [stage[:, 0, :], stage[:, 1, :]] + [
            probs_t[:, HPG * i:HPG * (i + 1), :].rearrange("p a q -> p (a q)") for i in range(2)]
        e_x_in = [sem(f"e_x_in{t}") for t in range(RING)]
        e_stored = [sem(f"e_stored{t}") for t in range(TT)]

        block = ctx.enter_context(nc.Block())

        def at(eng, s, per, b, k):
            if isinstance(b, int):
                if per * b + k > 0:
                    eng.wait_ge(s, per * b + k)
            else:
                eng.wait_ge(s, b * per + k)
                if eng is nc.sync:
                    unregistered(eng)

        def unregistered(eng):
            eng.sem_inc(passed, 1)

        def bodies(eng, body):
            body(0, attn_kinds, None)
            body(1, attn_kinds + cell_kinds, 0)
            with eng.Fori(2, B) as b:
                body(b, attn_kinds + cell_kinds, b - 1)
            body(B, cell_kinds, B - 1)

        def exists(b, t):
            return not isinstance(b, int) or 0 <= RING * b + t < TT * B

        def tile_of(b, t):
            return b + t // RING, t % RING

        def tiles(eng, step):
            rounds = TT * B // RING
            for t in range(-AHEAD_X1, RING):
                step(0, t)
            with eng.Fori(1, rounds - 1) as b:
                for t in range(RING):
                    step(b, t)
            for t in range(RING + 2):
                step(rounds - 1, t)

        @block.sync
        def _(sp):
            x_v = x_by_d.rearrange("b (t p) (g c) -> b t p g c", p=P, c=P)

            def load_x(b):
                at(sp, projected, TT, b, 0)
                for t in range(TT):
                    sp.dma_start(xa[:, :, t * P:(t + 1) * P], x_v[b, t]).then_inc(x_in[t], DMA)

            def body(b, kinds, _):
                first = isinstance(b, int) and b == 0
                for kind, n in steps:
                    if kind not in kinds:
                        continue
                    if kind == "norm1":
                        load_x(b)
                    if kind == "keys":
                        g = n
                        at(sp, k_lo, G, b, g + 1)
                        at(sp, k_stacked, DMA * G, b, DMA * g)
                        sp.dma_start(k_parts.rearrange("s d h t -> (d h) s t"), stage[:, :, :]).then_inc(k_out, DMA)
                        at(sp, k_out, DMA * G, b, DMA * (g + 1))
                        at(sp, scored, 2 * SLOTS, b, 2 * TT * (g - 1))
                        rows = k_parts.rearrange("s d h t -> (s d) (h t)").unsqueeze(0)
                        sp.dma_start(key_stack[:, g % 2].rearrange("p h t -> p (h t)").bitcast(F32),
                                     rows.to_broadcast([2, 2 * HEAD, HPG * T])).then_inc(k_stacked, DMA)
                    if kind == "queries":
                        g = n
                        at(sp, q_lo, G, b, g + 1)
                        for landed in q_stacked:
                            at(sp, landed, NSTACK * G, b, NSTACK * g)
                        for half_ in range(2):
                            sp.dma_start(q_parts[half_].rearrange("s d h t -> (d h) s t"),
                                         stage[:, :, half_ * T // 2:(half_ + 1) * T // 2]).then_inc(q_out[half_], DMA)
                        for half_ in range(2):
                            at(sp, q_out[half_], DMA * G, b, DMA * (g + 1))
                            at(sp, scored, 2 * SLOTS, b, 2 * (TT * (g - 1) + TT // 2 * (half_ + 1)))
                            cols = slice(half_ * T // 2, (half_ + 1) * T // 2)
                            for part in range(2):
                                rows = q_parts[half_, part].rearrange("d h t -> d (h t)").unsqueeze(0)
                                sp.dma_start(query_stack[2 * HEAD * part:2 * HEAD * (part + 1), :, cols].bitcast(F32),
                                             rows.to_broadcast([2, HEAD, HPG * T // 2])).then_inc(q_stacked[half_], DMA)
                        if first and g == 0:
                            load_weights(0, G)
                    if kind == "value" and first and n < SLOTS - TT:
                        s = n
                        load_weights(WPS * s + G, min(WPS * (s + 1) + G, NCH))
                    if kind == "weights":
                        at(sp, turned, 2 * SLOTS, b, 2 * SLOTS)
                        sp.dma_start(probs_w, w_proj.rearrange("(k p) n -> p k n", p=P)).then_inc(proj_in, DMA)
                        load_row(b, 0)
                        load_row(b, 1)
                    if kind == "norm2":
                        at(sp, x1_done, TT, b, n + 1)
                        sp.dma_start(x1_dram[b, n * P:(n + 1) * P, :], xr[:, n % 2, :]).then_inc(x1_out[n % 2], DMA)
                        if n + 2 < TT:
                            load_row(b, n + 2)

            def load_row(b, t):
                at(sp, x1_out[t % 2], DMA * TT // 2, b, DMA * (t // 2))
                at(sp, x2_done, TT, b, t - 1)
                sp.dma_start(xr[:, t % 2, :], x[b, t * P:(t + 1) * P, :]).then_inc(xr_in[t % 2], DMA)

            def load_weights(n0, n1):
                for n in range(n0, n1):
                    at(sp, w_lo, 0, 0, n - G + 1)
                    gt, u, k = chunks[n]
                    sp.dma_start(state[:, n % G, :], (u_gates if u else w_gates)[gt][k * P:(k + 1) * P, :])\
                      .then_inc(w_in[n % G], DMA)

            for gt in range(NG):
                sp.dma_start(bias[:, gt, :], biases[gt]).then_inc(const_in, DMA)
            sp.dma_start(c0[:, :], in_c).then_inc(const_in, DMA)
            sp.dma_start(bp_row[:, :], b_proj.partition_broadcast(P)).then_inc(bp_in, DMA)
            bodies(sp, body)

            at(sp, projected, TT, B, 0)
            sp.dma_start(wo_raw[:, :, :], w_out.rearrange("(k p) n -> p k n", p=P)).then_inc(e["raw_in"], DMA)
            sp.dma_start(uo_raw, u_out.rearrange("(k p) n -> p k n", p=P)).then_inc(e["raw_in"], DMA)
            at(sp, xr_ready, TT, B, 0)
            sp.dma_start(bp_row[:, :], b_out.partition_broadcast(P)).then_inc(e["bo_in"], DMA)
            for stored in x1_out:
                at(sp, stored, DMA * TT // 2, B, 0)
            at(sp, gate_sum, UNITS, B, -1)
            x1_v = x1_dram.rearrange("(r c) (t p) n -> r (c t) p n", c=RING // TT, p=P)
            out_v = out.rearrange("(r c) (t p) n -> r (c t) p n", c=RING // TT, p=P)

            def last(b, t):
                if exists(b, t + AHEAD_X1):
                    at(sp, e["out"], RING, b, t + AHEAD_X1 - RING + 1)
                    br, tr = tile_of(b, t + AHEAD_X1)
                    sp.dma_start(x1_ring[:, tr, :], x1_v[br, tr]).then_inc(e_x_in[tr], DMA)
                if exists(b, t - 1):
                    at(sp, e["out"], RING, b, t)
                    br, tr = tile_of(b, t - 1)
                    sp.dma_start(out_v[br, tr], h_ring[tr % TT]).then_inc(e_stored[tr % TT], DMA)

            tiles(sp, last)
            for stored in e_stored:
                sp.wait_ge(stored, DMA * B)

        @block.gpsimd
        def _(pool):
            pool.memset(ident[:, :], 0.0).then_inc(consts, 1)
            pool.memset(mask[:, :], 0.0).then_inc(consts, 1)
            pool.memset(half[:, :], -0.5).then_inc(consts, 1)
            pool.wait_ge(consts, 3)
            pool.affine_select(out=ident[:, :], in_=ident[:, :], compare_op=ALU.not_equal, fill=1.0,
                               base=0, pattern=[[-1, P]], channel_multiplier=1).then_inc(consts, 1)
            pool.affine_select(out=mask[:, :], in_=mask[:, :], compare_op=ALU.is_ge, fill=NEG,
                               base=-WINDOW, pattern=[[1, MASKW]], channel_multiplier=-1).then_inc(consts, 1)
            pool.wait_ge(consts, 5)
            pool.affine_select(out=mask[:, :], in_=mask[:, :], compare_op=ALU.is_ge, fill=NEG,
                               base=3 * WINDOW, pattern=[[-1, MASKW]], channel_multiplier=1).then_inc(consts, 1)
            pool.wait_ge(bp_in, DMA)

            def body(b, kinds, _):
                def add_bias(t):
                    at(pool, xr_in[t % 2], DMA * TT // 2, b, DMA * (t // 2 + 1))
                    pool.tensor_tensor(xr[:, t % 2, :], xr[:, t % 2, :], bp_row[:, :], ALU.add)\
                        .then_inc(xr_ready, 1)

                for kind, n in steps:
                    if kind not in kinds:
                        continue
                    if kind == "keys":
                        g = n
                        for left in q_out:
                            at(pool, left, DMA * G, b, DMA * g)
                        if not isinstance(b, int):
                            unregistered(pool)
                        pool.dma_start(stage_lo, ctx_t[b, g * P:(g + 1) * P, :].rearrange("(h d) t -> d h t", h=HPG)).then_inc(k_in, DMA)
                        at(pool, valued, SLOTS, b, TT * (g - 1))
                        if not isinstance(b, int):
                            unregistered(pool)
                        rows = ctx_rows[b].rearrange("(t p) c -> p t c", p=P)
                        pool.dma_start(values[:, g % 2, 0:TT, :],
                                     rows[:, :, g * P:(g + 1) * P]).then_inc(v_in[g % 2], DMA)
                        rows = ctx_rows[b, WINDOW:T - WINDOW, :].rearrange("(t p) c -> p t c", p=P)
                        pool.dma_start(values[:, g % 2, TT:NV, :],
                                     rows[:, :, g * P:(g + 1) * P]).then_inc(v_in[g % 2], DMA)
                    if kind == "keys" and n == 0:
                        at(pool, var1, 1, b, 1)
                        pool.tensor_tensor(rs1[:, :], ve1[:, :], half[:, :], ALU.pow).then_inc(rstd1, 1)
                    if kind == "proj" and n == 0:
                        add_bias(0)
                        add_bias(1)
                    if kind == "norm2":
                        t = n
                        at(pool, var2, TT, b, t + 1)
                        pool.tensor_tensor(rs2[:, :], ve2[:, :], half[:, 0:1], ALU.pow).then_inc(rstd2, 1)
                        if t + 2 < TT:
                            add_bias(t + 2)

            bodies(pool, body)

            def last(b, t):
                if exists(b, t + 2):
                    at(pool, e["var"], RING, b, t + 3)
                    pool.tensor_tensor(rs2[:, :], ve2[:, :], half[:, 0:1], ALU.pow).then_inc(e["rstd"], 1)
                if exists(b, t - 1):
                    at(pool, e["tanh"], RING, b, t)
                    _, tr = tile_of(b, t - 1)
                    row = h_ring[tr % TT]
                    pool.tensor_tensor(row, row, x1_ring[:, tr, :], ALU.add).then_inc(e["out"], 1)

            tiles(pool, last)

        @block.tensor
        def _(pe):
            def product(ps, lhs, rhs, start, stop):
                pe.matmul(ps, lhs[0], rhs[0], start=start, stop=False)
                pe.matmul(ps, lhs[0], rhs[1], start=False, stop=False)
                return pe.matmul(ps, lhs[1], rhs[0], start=False, stop=stop)

            def quarter(u, h):
                m, gt = u // NG, u % NG
                is_u = h < G // 2
                hi, lo = (state_hi, state_lo) if is_u else (x2t_hi, x2t_lo)
                for k in range(G // 2 * (h % 2), G // 2 * (h % 2 + 1)):
                    w = gate_w[:, gt, 1 if is_u else 0, :, k, m * P:(m + 1) * P]
                    mm = product(ps_d[u % 2][:, :], (w[:, 0, :], w[:, 1, :]), (hi[:, k, :], lo[:, k, :]),
                                 h == 0 and k == 0, h == G - 1 and k == G - 1)
                return mm

            pe.wait_ge(consts, 4)

            def body(b, kinds, bc):
                first = isinstance(b, int) and b == 0
                for kind, n in steps:
                    if kind not in kinds:
                        continue
                    if kind == "queries":
                        g = n
                        if g == 0:
                            at(pe, ln1, TT, b, TT)
                            at(pe, x2_lo, TT, b, 0)
                        elif g == 1:
                            at(pe, q_lo, G, b, 1)
                        else:
                            at(pe, recip_out, G, b, g - 1)
                        for t in range(TT):
                            mm = pe.transpose(ps_x[:, t * P:(t + 1) * P],
                                              xa[:, g, t * P:(t + 1) * P],
                                              ident[:, :])
                        mm.then_inc(q_turned, 1)
                    elif kind == "score":
                        g, t = n // TT, n % TT
                        if t == 0:
                            at(pe, k_stacked, DMA * G, b, DMA * (g + 1))
                        if t % 2 == 0:
                            at(pe, q_stacked[t // 2], NSTACK * G, b, NSTACK * (g + 1))
                        if n == 0:
                            at(pe, x1_done, TT, b, 0)
                        for h in range(HPG):
                            if h % 2 == 0:
                                at(pe, masked, HPG * SLOTS, b, HPG * n - 2 + h)
                            mm = pe.matmul(ps_s[h // 2][:, (h % 2) * KEYS:(h % 2 + 1) * KEYS],
                                           query_stack[:, h, t * P:(t + 1) * P],
                                           key_stack[:, g % 2, h, KEY0[t]:KEY0[t] + KEYS],
                                           start=True, stop=True)
                            if h % 2 == 1:
                                mm.then_inc(scored, 1)
                    elif kind == "turn":
                        if n == 0:
                            at(pe, x1_done, TT, b, 0)
                        for h in range(HPG):
                            at(pe, expd, HPG * SLOTS, b, HPG * n + h + 1)
                            if h == 0:
                                at(pe, turned_a, SLOTS, b, n)
                            if h == 2:
                                at(pe, turned_b, SLOTS, b, n)
                            for c in range(2):
                                at_ = ((h % 2) * 2 + c) * P
                                mm = pe.transpose(ps_t[h // 2][:, at_:at_ + P],
                                                  probs[:, n % 2, h, c * P:(c + 1) * P], ident[:, :])
                            if h % 2 == 1:
                                mm.then_inc(turned, 1)
                    elif kind == "value":
                        g, t = n // TT, n % TT
                        at(pe, turned_a, SLOTS, b, n + 1)
                        at(pe, turned_b, SLOTS, b, n + 1)
                        if t == 0:
                            at(pe, attn_t, G, b, g)
                            at(pe, x2_lo, TT, b, 0)
                            v_count = DMA * G
                            at(pe, v_in[g % 2], v_count, b, DMA * 2 * (g // 2 + 1))
                        for c in range(2):
                            for h in range(HPG):
                                mm = pe.matmul(ps_v[HEAD * h:HEAD * (h + 1), t * P:(t + 1) * P],
                                               values[:, g % 2, VTILES[t][c], HEAD * h:HEAD * (h + 1)],
                                               probs_t[:, 2 * h + c, :], start=(c == 0), stop=(c == 1))
                        mm.then_inc(valued, 1)
                    elif kind == "norm":
                        g = n
                        at(pe, inv, SLOTS, b, TT * (g + 1))
                        if g == 3:
                            at(pe, recip_out, G, b, 3)
                        else:
                            at(pe, q_lo, G, b, g + 2)
                        for t in range(TT):
                            mm = pe.transpose(ps_x[:, t * P:(t + 1) * P],
                                              recip[:, t, :],
                                              ident[:, :])
                        mm.then_inc(spread, 1)
                    elif kind == "proj":
                        t = n
                        if t == 0:
                            at(pe, attn_t, G, b, G)
                            at(pe, proj_in, DMA, b, DMA)
                            at(pe, masked, HPG * SLOTS, b, HPG * SLOTS)
                            at(pe, turned_a, SLOTS, b, SLOTS)
                            at(pe, turned_b, SLOTS, b, SLOTS)
                        for k in range(G):
                            mm = pe.matmul(ps_proj[t][:, :], xa[:, k, t * P:(t + 1) * P], probs_w[:, k, :],
                                           start=(k == 0), stop=(k == G - 1))
                        mm.then_inc(projected, 1)
                    elif kind == "turn2":
                        t = n
                        at(pe, x2_done, TT, b, t + 1)
                        if t == 0:
                            at(pe, recip_out, G, b, G)
                        if t >= 2:
                            at(pe, x2_lo, TT, b, t - 1)
                        for k in range(G):
                            mm = pe.transpose(ps_turn2[t % 2][:, k * P:(k + 1) * P], x2_at(t)[:, k * P:(k + 1) * P],
                                              ident[:, :])
                        mm.then_inc(x2_turned, 1)
                    elif kind == "ahead":
                        u, h = n
                        if n == (0, 0):
                            if first:
                                pe.wait_ge(w_lo, NCH)
                            at(pe, c_hi, G, b, G)
                            at(pe, c_lo, G, b, G)
                        if h == 0:
                            at(pe, gated, UNITS, b, 0)
                        quarter(u, h)
                    elif kind == "cell":
                        u, h = n
                        if n == quarters[0]:
                            at(pe, x2_lo, TT, bc, TT)
                            at(pe, x2_hi, TT, bc, TT)
                        if h == 0:
                            at(pe, gated, UNITS, bc, u - 1)
                        mm = quarter(u, h)
                        if h == G - 1:
                            mm.then_inc(gate_sum, 1)

            bodies(pe, body)

            pe.wait_ge(e["lo"], 2 * G)
            pe.wait_ge(e["hi"], 2 * G)
            at(pe, c_lo, G, B, G)
            for t in range(TT):
                for k in range(G):
                    mm = product(ps_proj[t][:, :], (state_hi[:, k, t * P:(t + 1) * P], state_lo[:, k, t * P:(t + 1) * P]),
                                 (uo_hi[:, k, :], uo_lo[:, k, :]), k == 0, k == G - 1)
                mm.then_inc(e["base_mm"], 1)

            def last(b, t):
                if exists(b, t):
                    tt = t % TT
                    at(pe, e["x2lo"], RING, b, t + 1)
                    at(pe, e["sum"], RING, b, t - 1)
                    for k in range(G):
                        mm = product(ps_d[t % 2][:, :],
                                     (x2t_hi[:, k, tt * P:(tt + 1) * P], x2t_lo[:, k, tt * P:(tt + 1) * P]),
                                     (wo_hi[:, k, :], wo_lo[:, k, :]), k == 0, k == G - 1)
                    mm.then_inc(e["mm"], 1)
                if exists(b, t + 2):
                    at(pe, e["x2"], RING, b, t + 3)
                    at(pe, e["x2lo"], RING, b, t + 1)
                    for k in range(G):
                        mm = pe.transpose(ps_turn2[t % 2][:, k * P:(k + 1) * P], x2_at(t)[:, k * P:(k + 1) * P],
                                          ident[:, :])
                    mm.then_inc(e["turned"], 1)

            tiles(pe, last)

        @block.scalar
        def _(act):
            def split_weights(n0, n1):
                for n in range(n0, n1):
                    gt, u, k = chunks[n]
                    act.wait_ge(w_in[n % G], DMA * (n // G + 1))
                    act.activation(gate_w[:, gt, u, 0, k, :], state[:, n % G, :], ACT.Copy,
                                   scale=0.5 if u else 1.0).then_inc(w_hi, 1)

            def split_out(j):
                act.wait_ge(e["raw_in"], 2 * DMA)
                out_, raw = (wo_hi, wo_raw) if j < G else (uo_hi, uo_raw)
                act.activation(out_[:, j % G, :], raw[:, j % G, :], ACT.Copy, scale=1.0 if j < G else 0.5)\
                   .then_inc(e["hi"], 1)

            def body(b, kinds, bc):
                first = isinstance(b, int) and b == 0
                for kind, n in steps:
                    if kind not in kinds:
                        continue
                    if kind == "keys":
                        g = n
                        at(act, k_in, DMA * G, b, DMA * (g + 1))
                        act.activation(stage_hi, stage_lo, ACT.Copy).then_inc(k_hi, 1)
                    elif kind == "queries":
                        g = n
                        at(act, q_turned, G, b, g + 1)
                        at(act, k_out, DMA * G, b, DMA * (g + 1))
                        act.activation(stage_hi, ps_x[:, :], ACT.Copy).then_inc(q_hi, 1)
                    elif kind == "exp":
                        at(act, nmax, SLOTS, b, n + 1)
                        for h in range(HPG):
                            at(act, inv, SLOTS, b, n - TT + 1)
                            row = probs[:, n % 2, h, :]
                            act.activation(row, row, ACT.Exp, bias=negmax[:, n % 2, h:h + 1], scale=SCALE,
                                           accum_out=rowsum[:, n % TT, h:h + 1]).then_inc(expd, 1)
                    elif kind == "turn":
                        at(act, turned, 2 * SLOTS, b, 2 * n + 1)
                        at(act, valued, SLOTS, b, n)
                        act.activation(probs_t[:, 0:HPG, :], ps_t[0][:, :].rearrange("p (a q) -> p a q", a=HPG),
                                       ACT.Copy).then_inc(turned_a, 1)
                    elif kind == "norm":
                        at(act, spread, G, b, n + 1)
                        at(act, attn_t, G, b, n)
                        at(act, x2_turned, TT, b, 0)
                        act.activation(recip_sb, ps_x[:, :], ACT.Copy).then_inc(recip_out, 1)
                    elif kind == "turn2":
                        t = n
                        at(act, x2_turned, TT, b, t + 1)
                        if t == 0 and bc is not None:
                            at(act, gate_sum, UNITS, bc, UNITS)
                        act.activation(x2t_hi[:, :, t * P:(t + 1) * P],
                                       ps_turn2[t % 2][:, :].rearrange("p (k q) -> p k q", k=G),
                                       ACT.Copy).then_inc(x2_hi, 1)
                    elif kind == "gate":
                        u = n
                        m, gt = u // NG, u % NG
                        if "proj" not in kinds and 2 <= u < 2 * G + 2:
                            split_out(u - 2)
                        at(act, gate_sum, UNITS, bc, u + 1)
                        if gt == 2:
                            at(act, in_gate, G, bc, m + 1)
                        else:
                            at(act, cell, G, bc, m)
                        act.activation(gate[:, min(gt, 1), :], ps_d[u % 2][:, :], ACT.Tanh, bias=bias[:, gt, m:m + 1],
                                       scale=1.0 if gt == 0 else 0.5).then_inc(gated, 1)
                    elif kind == "state":
                        for m in range(G):
                            at(act, cell, G, bc, m + 1)
                            at(act, gate_sum, UNITS, bc, UNITS)
                            act.activation(state_hi[:, m, :], state[:, m, :], ACT.Copy).then_inc(c_hi, 1)
                    if first and kind == "value" and n < SLOTS - TT:
                        split_weights(WPS * n, WPS * (n + 1))
                    if first and kind == "value" and n >= SLOTS - TT:
                        m = n - (SLOTS - TT)
                        act.wait_ge(c_init, 2 * m + 2)
                        act.activation(state_hi[:, m, :], state[:, m, :], ACT.Copy).then_inc(c_hi, 1)
                        act.wait_ge(bias_half, 1)

            bodies(act, body)

            def last(b, t):
                if exists(b, t - 1):
                    row = h_ring[(t - 1) % TT]
                    at(act, e["sum"], RING, b, t)
                    act.activation(row, row, ACT.Tanh).then_inc(e["tanh"], 1)
                if exists(b, t + 2):
                    tt = (t + 2) % TT
                    at(act, e["turned"], RING, b, t + 3)
                    at(act, e["mm"], RING, b, t - 1)
                    act.activation(x2t_hi[:, :, tt * P:(tt + 1) * P],
                                   ps_turn2[t % 2][:, :].rearrange("p (k q) -> p k q", k=G),
                                   ACT.Copy).then_inc(e["x2hi"], 1)

            tiles(act, last)

        @block.vector
        def _(dve):
            dve.wait_ge(const_in, DMA * (NG + 1))
            dve.tensor_scalar(bias[:, 1:NG, :], bias[:, 1:NG, :], 0.5, None, ALU.mult).then_inc(bias_half, 1)
            dve.wait_ge(consts, 6)

            def split_weights(n0, n1):
                for n in range(n0, n1):
                    gt, u, k = chunks[n]
                    dve.wait_ge(w_hi, n + 1)
                    dve.scalar_tensor_tensor(out=gate_w[:, gt, u, 1, k, :], in0=state[:, n % G, :],
                                             scalar=0.5 if u else 1.0,
                                             in1=gate_w[:, gt, u, 0, k, :].bitcast(F32),
                                             op0=ALU.mult, op1=ALU.subtract).then_inc(w_lo, 1)

            def body(b, kinds, bc):
                first = isinstance(b, int) and b == 0
                def norm1():
                    for t in range(TT):
                        at(dve, x_in[t], DMA, b, DMA)
                        dve.bn_stats(st1[:, t, :], xa[:, :, t * P:(t + 1) * P]).then_inc(stat1, 1)
                    for t in range(TT):
                        at(dve, stat1, TT, b, t + 1)
                        unregistered(dve)
                        dve.bn_aggr(mv1[:, t, :], st1[:, t, :]).then_inc(aggr1, 1)
                    at(dve, aggr1, TT, b, TT)
                    dve.tensor_scalar(ve1[:, :], mv1[:, :, 1], EPS, None, ALU.add).then_inc(var1, 1)
                    at(dve, rstd1, 1, b, 1)
                    for t in range(TT):
                        tile = xa[:, :, t * P:(t + 1) * P]
                        dve.tensor_scalar(tile, tile, mv1[:, t, 0:1], rs1[:, t:t + 1], ALU.subtract, ALU.mult)\
                           .then_inc(ln1, 1)
                for kind, n in steps:
                    if kind not in kinds:
                        continue
                    if kind == "norm1":
                        norm1()
                    elif kind == "keys":
                        g = n
                        at(dve, k_hi, G, b, g + 1)
                        dve.tensor_tensor(stage_lo, stage_lo, stage[:, 0, :],
                                          ALU.subtract).then_inc(k_lo, 1)
                    elif kind == "queries":
                        g = n
                        at(dve, q_hi, G, b, g + 1)
                        dve.tensor_tensor(stage_lo, ps_x[:, :], stage[:, 0, :],
                                          ALU.subtract).then_inc(q_lo, 1)
                    elif kind == "score":
                        g, t = n // TT, n % TT
                        at(dve, turned, 2 * SLOTS, b, 2 * (n - 1))
                        for h in range(HPG):
                            if h % 2 == 0:
                                at(dve, scored, 2 * SLOTS, b, 2 * n + h // 2 + 1)
                                unregistered(dve)
                            dve.tensor_tensor_reduce(probs[:, n % 2, h, :],
                                                     ps_s[h // 2][:, (h % 2) * KEYS:(h % 2 + 1) * KEYS],
                                                     mask[:, MASK0[t]:MASK0[t] + KEYS], 1.0, NEG,
                                                     ALU.add, ALU.max, rowmax[:, n % 2, h:h + 1]).then_inc(masked, 1)
                        at(dve, masked, HPG * SLOTS, b, HPG * (n + 1))
                        dve.tensor_scalar(negmax[:, n % 2, :], rowmax[:, n % 2, :], -SCALE, None, ALU.mult)\
                           .then_inc(nmax, 1)
                    elif kind == "turn":
                        at(dve, turned, 2 * SLOTS, b, 2 * n + 2)
                        at(dve, valued, SLOTS, b, n)
                        dve.tensor_copy(probs_t[:, HPG:2 * HPG, :], ps_t[1][:, :].rearrange("p (a q) -> p a q", a=HPG))\
                           .then_inc(turned_b, 1)
                        at(dve, spread, G, b, n // TT)
                        at(dve, x2_turned, TT, b, 0)
                        dve.reciprocal(rowsum[:, n % TT, :], rowsum[:, n % TT, :]).then_inc(inverted, 1)
                        at(dve, inverted, SLOTS, b, n + 1)
                        dve.tensor_copy(recip[:, n % TT, :].rearrange("p (h d) -> p h d", h=HPG),
                                        rowsum[:, n % TT, :].unsqueeze(2).to_broadcast([P, HPG, HEAD])).then_inc(inv, 1)
                    elif kind == "norm":
                        at(dve, recip_out, G, b, n + 1)
                        at(dve, valued, SLOTS, b, TT * (n + 1))
                        dve.tensor_tensor(xa[:, n, :], ps_v[:, :], recip_sb, ALU.mult).then_inc(attn_t, 1)
                    elif kind == "proj":
                        t = n
                        at(dve, projected, TT, b, t + 1)
                        at(dve, xr_ready, TT, b, t + 1)
                        row = xr[:, t % 2, :]
                        dve.tensor_tensor(row, ps_proj[t][:, :], row, ALU.add).then_inc(x1_done, 1)
                        stats2(b, t)
                    elif kind == "norm2":
                        norm2(b, n)
                    elif kind == "turn2":
                        t = n
                        at(dve, x2_hi, TT, b, t + 1)
                        dve.tensor_tensor(x2t_lo[:, :, t * P:(t + 1) * P],
                                          ps_turn2[t % 2][:, :].rearrange("p (k q) -> p k q", k=G),
                                          x2t_hi[:, :, t * P:(t + 1) * P].bitcast(F32),
                                          ALU.subtract).then_inc(x2_lo, 1)
                    elif kind == "gate":
                        u = n
                        m, gt = u // NG, u % NG
                        if "proj" not in kinds and 2 <= u < G + 2:
                            split_out(u - 2)
                        at(dve, gated, UNITS, bc, u + 1)
                        if "proj" not in kinds and u == UNITS - NG + 1:
                            for j in range(G, 2 * G):
                                split_out(j)
                        if gt == 1:
                            dve.scalar_tensor_tensor(out=gate[:, 0, :], in0=gate[:, 1, :], scalar=1.0, in1=gate[:, 0, :],
                                                     op0=ALU.add, op1=ALU.mult).then_inc(in_gate, 1)
                        if gt == 2:
                            dve.scalar_tensor_tensor(out=gate[:, 1, :], in0=gate[:, 1, :], scalar=1.0, in1=state[:, m, :],
                                                     op0=ALU.add, op1=ALU.mult).then_inc(kept, 1)
                            at(dve, kept, G, bc, m + 1)
                            at(dve, in_gate, G, bc, m + 1)
                            dve.scalar_tensor_tensor(out=state[:, m, :], in0=gate[:, 1, :], scalar=0.5, in1=gate[:, 0, :],
                                                     op0=ALU.mult, op1=ALU.add).then_inc(cell, 1)
                    elif kind == "state":
                        for m in range(G):
                            at(dve, c_hi, G, bc, G + m + 1)
                            dve.tensor_tensor(state_lo[:, m, :], state[:, m, :], state_hi[:, m, :].bitcast(F32),
                                              ALU.subtract).then_inc(c_lo, 1)
                    if first and kind == "value" and n < SLOTS - TT:
                        split_weights(WPS * n, WPS * (n + 1))
                    if first and kind == "value" and n >= SLOTS - TT:
                        m = n - (SLOTS - TT)
                        dve.wait_ge(w_lo, NCH)
                        dve.memset(state[:, m, :], 0.0).then_inc(c_init, 1)
                        dve.wait_ge(c_init, 2 * m + 1)
                        dve.tensor_scalar(state[:, m, :], state[:, m, :], c0[:, m:m + 1], 2.0, ALU.add, ALU.mult)\
                           .then_inc(c_init, 1)
                        dve.wait_ge(c_hi, m + 1)
                        dve.tensor_tensor(state_lo[:, m, :], state[:, m, :], state_hi[:, m, :].bitcast(F32),
                                          ALU.subtract).then_inc(c_lo, 1)

            def split_out(j):
                dve.wait_ge(e["hi"], j + 1)
                if j == G:
                    at(dve, gate_sum, UNITS, B - 1, UNITS - NG + 1)
                hi, lo, raw = (wo_hi, wo_lo, wo_raw) if j < G else (uo_hi, uo_lo, uo_raw)
                dve.scalar_tensor_tensor(out=lo[:, j % G, :], in0=raw[:, j % G, :], scalar=1.0 if j < G else 0.5,
                                         in1=hi[:, j % G, :].bitcast(F32), op0=ALU.mult, op1=ALU.subtract)\
                   .then_inc(e["lo"], 1)

            def stats2(b, t):
                row = xr[:, t % 2, :]
                at(dve, x1_done, TT, b, t + 1)
                dve.bn_stats(st2[:, :], row).then_inc(stat2, 1)
                at(dve, stat2, TT, b, t + 1)
                unregistered(dve)
                dve.bn_aggr(mv2[:, :], st2[:, :]).then_inc(aggr2, 1)
                at(dve, aggr2, TT, b, t + 1)
                dve.tensor_scalar(ve2[:, :], mv2[:, 1:2], EPS, None, ALU.add).then_inc(var2, 1)

            def norm2(b, t):
                row = xr[:, t % 2, :]
                at(dve, rstd2, TT, b, t + 1)
                at(dve, x2_turned, TT, b, t - 1)
                dve.tensor_scalar(x2_at(t), row, mv2[:, 0:1], rs2[:, 0:1], ALU.subtract, ALU.mult).then_inc(x2_done, 1)

            bodies(dve, body)

            def base():
                dve.wait_ge(e["bo_in"], DMA)
                for t in range(TT):
                    dve.wait_ge(e["base_mm"], t + 1)
                    dve.tensor_tensor(state[:, t, :], ps_proj[t][:, :], bp_row[:, :], ALU.add).then_inc(e["base"], 1)

            def last(b, t):
                if isinstance(b, int) and RING * b + t == 0:
                    base()
                if exists(b, t + 2):
                    br, tr = tile_of(b, t + 2)
                    row = x1_ring[:, tr, :]
                    at(dve, e_x_in[tr], DMA, br, DMA)
                    dve.bn_stats(st2[:, :], row).then_inc(e["stat"], 1)
                    at(dve, e["stat"], RING, b, t + 3)
                    unregistered(dve)
                    dve.bn_aggr(mv2[:, :], st2[:, :]).then_inc(e["aggr"], 1)
                    at(dve, e["aggr"], RING, b, t + 3)
                    dve.tensor_scalar(ve2[:, :], mv2[:, 1:2], EPS, None, ALU.add).then_inc(e["var"], 1)
                if exists(b, t - 1):
                    br, tr = tile_of(b, t - 1)
                    at(dve, e["mm"], RING, b, t)
                    at(dve, e["base"], 0, 0, TT)
                    at(dve, e_stored[tr % TT], DMA * (RING // TT), br, DMA * (tr // TT))
                    dve.tensor_tensor(h_ring[tr % TT], ps_d[(t - 1) % 2][:, :], state[:, tr % TT, :], ALU.add)\
                       .then_inc(e["sum"], 1)
                if exists(b, t + 1):
                    tt = (t + 1) % TT
                    at(dve, e["x2hi"], RING, b, t + 2)
                    dve.tensor_tensor(x2t_lo[:, :, tt * P:(tt + 1) * P],
                                      ps_turn2[(t + 1) % 2][:, :].rearrange("p (k q) -> p k q", k=G),
                                      x2t_hi[:, :, tt * P:(tt + 1) * P].bitcast(F32),
                                      ALU.subtract).then_inc(e["x2lo"], 1)
                if exists(b, t + 2):
                    at(dve, e["rstd"], RING, b, t + 3)
                    at(dve, e["turned"], RING, b, t + 1)
                    dve.tensor_scalar(x2_at(t), row, mv2[:, 0:1], rs2[:, 0:1], ALU.subtract, ALU.mult)\
                       .then_inc(e["x2"], 1)

            tiles(dve, last)


def kernel(x, ctx_1024, L0_xattn_W_proj, L0_xattn_b_proj, L0_ffn_wf, L0_ffn_uf, L0_ffn_bf, L0_ffn_wi,
           L0_ffn_ui, L0_ffn_bi, L0_ffn_wc, L0_ffn_uc, L0_ffn_bc, L0_ffn_wo, L0_ffn_uo, L0_ffn_bo, L0_ffn_in_c):
    import numpy as np
    import concourse.bacc as bacc
    from concourse.bass_utils import run_bass_kernel_spmd

    def transposed(a):
        return np.ascontiguousarray(np.swapaxes(np.asarray(a), -1, -2))

    def columns(a):
        return np.ascontiguousarray(np.asarray(a).reshape(-1, P).T)

    arrays = {
        "x": np.ascontiguousarray(x),
        "x_by_d": transposed(np.asarray(x).reshape(*x.shape[:2], -1, HPG, HEAD)).reshape(x.shape),
        "ctx_rows": np.ascontiguousarray(ctx_1024), "ctx_t": transposed(ctx_1024),
        "w_proj": transposed(L0_xattn_W_proj), "b_proj": np.ascontiguousarray(L0_xattn_b_proj),
        "w_c": transposed(L0_ffn_wc), "w_i": transposed(L0_ffn_wi), "w_f": transposed(L0_ffn_wf),
        "u_c": transposed(L0_ffn_uc), "u_i": transposed(L0_ffn_ui), "u_f": transposed(L0_ffn_uf),
        "b_c": columns(L0_ffn_bc), "b_i": columns(L0_ffn_bi), "b_f": columns(L0_ffn_bf),
        "w_out": transposed(L0_ffn_wo), "u_out": transposed(L0_ffn_uo), "b_out": np.ascontiguousarray(L0_ffn_bo),
        "in_c": columns(L0_ffn_in_c),
    }
    nc = bacc.Bacc("TRN2", target_bir_lowering=False, num_devices=1)
    d = {n: nc.dram_tensor(n, a.shape, mybir.dt.from_np(a.dtype), kind="ExternalInput").ap()
         for n, a in arrays.items()}
    out = nc.dram_tensor("out", arrays["x"].shape, F32, kind="ExternalOutput").ap()
    x1_dram = nc.dram_tensor("x1_dram", arrays["x"].shape, F32, kind="Internal").ap()
    T = arrays["x"].shape[1]
    k_parts = nc.dram_tensor("k_parts", (2, HEAD, HPG, T), F32, kind="Internal").ap()
    q_parts = nc.dram_tensor("q_parts", (2, 2, HEAD, HPG, T // 2), F32, kind="Internal").ap()
    bass_xattn_ffn(nc, d["x"], d["x_by_d"], d["ctx_rows"], d["ctx_t"], d["w_proj"], d["b_proj"],
                   [d["w_c"], d["w_i"], d["w_f"]], [d["u_c"], d["u_i"], d["u_f"]],
                   [d["b_c"], d["b_i"], d["b_f"]], d["w_out"], d["u_out"], d["b_out"], d["in_c"], out, x1_dram,
                   k_parts, q_parts)
    r = run_bass_kernel_spmd(nc, [arrays], core_ids=[0])
    return r.results[0]["out"]
```
